# Optimizing a Trainium2 kernel written in Bass

```python
import numpy as np
import jax
import jax.numpy as jnp

def _softmax(x, axis=-1):
    return jax.nn.softmax(x, axis=axis)

def _gelu(x):
    return jax.nn.gelu(x, approximate=True)

def _silu(x):
    return jax.nn.silu(x)

def _sigmoid(x):
    return jax.nn.sigmoid(x)

def _layernorm(x, axis=-1, eps=1e-05):
    m = jnp.mean(x, axis=axis, keepdims=True)
    v = jnp.var(x, axis=axis, keepdims=True)
    return (x - m) / jnp.sqrt(v + eps)

def _scatter_add(tgt, idx, src, axis=0):
    return tgt.at[idx].add(src)

def _segment_sum(src, seg, n):
    return jax.ops.segment_sum(src, seg, n)
kernel_name = 'mk_xattn_ffn_d1_seqx_r2_5da952'

def setup_inputs(seed: int=0):
    np.random.seed(seed)
    _w = jnp.asarray

    def _rec_inputs():
        import jax
        import jax.numpy as jnp
        _rk = jax.random.key(seed)
        x = -0.0003929 + 0.9999 * jax.random.normal(jax.random.fold_in(_rk, 1), (16, 512, 512), jnp.float32)
        _lenS = 512 - jax.random.randint(jax.random.fold_in(_rk, 7), (16,), 0, max(1, 512 // 4) + 1, jnp.int32)
        _lenS2 = 512 - jax.random.randint(jax.random.fold_in(_rk, 8), (16,), 0, max(1, 512 // 4) + 1, jnp.int32)
        _ctx_2048P = jax.random.normal(jax.random.fold_in(_rk, 11), (16, 16, 1024), jnp.float32)
        _ctx_2048c = jax.random.dirichlet(jax.random.fold_in(_rk, 511), 0.3 * jnp.ones((16,), jnp.float32), (16, 512))
        _ctx_2048t = jnp.einsum('bsk,bkd->bsd', _ctx_2048c, _ctx_2048P)
        _ctx_2048t = _ctx_2048t * jax.lax.rsqrt(jnp.mean(jnp.square(_ctx_2048t)) + 1e-12) * 0.953939
        ctx_2048 = 4.13588e-05 + 0.999923 * (_ctx_2048t + 0.3 * jax.random.normal(jax.random.fold_in(_rk, 611), (16, 512, 1024), jnp.float32))
        _validS = jnp.arange(512)[None, :] < _lenS[:, None]
        _validS2 = jnp.arange(512)[None, :] < _lenS2[:, None]
        _causal = jnp.tril(jnp.ones((512, 512), dtype=bool))
        mask_BxS2_if0 = jnp.where(jnp.ones((16, 512), dtype=bool), 4, 0).astype(jnp.int32)
        return (x, ctx_2048, mask_BxS2_if0)
    x, ctx_2048, mask_BxS2_if0 = _rec_inputs()

    def _L0_xattn_setup():
        import jax, jax.numpy as jnp
        import numpy as np
        B, L, P = (4, 2048, 512)
        D_MODEL = 512
        D_GLOBAL = 1024
        HEADDIM = 32
        EPSILON = 0.001
        RMS_EPS = 1e-05

        def rmsnorm(x, g, eps=RMS_EPS):
            var = jnp.mean(jnp.square(x), axis=-1, keepdims=True)
            return x * jax.lax.rsqrt(var + eps) * g

        def _hnet_depool(h, h_patch_full, patch_lens):
            h_patch = h_patch_full[..., :D_MODEL]
            bsz, plen = (h_patch.shape[0], h_patch.shape[1])
            seqlen = h.shape[1]
            logp = jnp.full((bsz, plen), -EPSILON, dtype=jnp.float32)
            bidx = jnp.cumsum(patch_lens, axis=1) - 1
            boundary_mask = jnp.zeros((bsz, seqlen), dtype=jnp.int32)
            boundary_mask = boundary_mask.at[jnp.arange(bsz)[:, None], bidx].set(1)
            dt = (-jnp.log(-jnp.expm1(logp))).astype(h_patch.dtype)
            x = h_patch / dt[..., None]
            n_heads = D_MODEL // HEADDIM
            A = -jnp.ones((n_heads,), dtype=jnp.float32)
            bcoef = jnp.exp(logp).astype(h_patch.dtype)
            x4 = x.reshape(bsz, plen, n_heads, HEADDIM)
            a = jnp.exp(dt[:, :, None] * A[None, None, :])
            u = (dt * bcoef)[:, :, None, None] * x4
            a_b = jnp.broadcast_to(a[..., None], u.shape)

            def comb(lft, rgt):
                aL, uL = lft
                aR, uR = rgt
                return (aL * aR, uL * aR + uR)
            _, s = jax.lax.associative_scan(comb, (a_b, u), axis=1)
            depool = s.reshape(bsz, plen, D_MODEL)
            plug = jnp.clip(jnp.cumsum(boundary_mask, axis=1) - 1, 0, plen - 1)
            depool_out = depool[jnp.arange(bsz)[:, None], plug]
            return depool_out + h
        key = jax.random.key(seed)
        k1, k2, k3, k4 = jax.random.split(key, 4)
        embeds = jax.random.normal(k1, (B, L, D_MODEL), dtype=jnp.float32)
        patch_embeds = jax.random.normal(k2, (B, P, D_GLOBAL), dtype=jnp.float32)
        patch_lens = jnp.full((B, P), L // P, dtype=jnp.int64)
        W_in = jax.random.normal(k3, (D_MODEL, D_MODEL), dtype=jnp.float32) * 0.02
        b_in = jnp.zeros((D_MODEL,), dtype=jnp.float32)
        g_res = jnp.ones((D_MODEL,), dtype=jnp.float32)
        g_init = jnp.ones((D_GLOBAL,), dtype=jnp.float32)
        return {'embeds': embeds, 'patch_embeds': patch_embeds, 'patch_lens': patch_lens, 'W_in': W_in, 'b_in': b_in, 'g_res': g_res, 'g_init': g_init}
    _L0_xattn_all = _L0_xattn_setup()
    _L0_xattn_in = {k: v for k, v in _L0_xattn_all.items() if k in ('W_in', 'b_in', 'g_res', 'g_init')}
    del _L0_xattn_all

    def _L0_ffn_setup():
        import jax, jax.numpy as jnp
        import numpy as np
        DIM = 512

        def _reference_tuple_inner(x, W_r, W_k, W_v, mu_r, mu_k):
            B, T, C = x.shape
            x_prev = jnp.concatenate([jnp.zeros((B, 1, C), x.dtype), x[:, :-1, :]], axis=1)
            xr = mu_r * x + (1.0 - mu_r) * x_prev
            xk = mu_k * x + (1.0 - mu_k) * x_prev
            r = jax.nn.sigmoid(jnp.einsum('btc,dc->btd', xr, W_r))
            k = jnp.einsum('btc,dc->btd', xk, W_k)
            k_act = jnp.square(jax.nn.relu(k))
            out = r * jnp.einsum('btc,dc->btd', k_act, W_v)
            new_state = x[:, -1, :]
            return (out, new_state)
        key = jax.random.key(seed)
        ks = jax.random.split(key, 6)
        B, T, C = (8, 1024, DIM)
        x = jax.random.normal(ks[0], (B, T, C), dtype=jnp.float32)
        s = 1.0 / np.sqrt(C)
        W_r = jax.random.uniform(ks[1], (C, C), jnp.float32, -s, s)
        W_k = jax.random.uniform(ks[2], (C, C), jnp.float32, -s, s)
        W_v = jax.random.uniform(ks[3], (C, C), jnp.float32, -s, s)
        mu_r = jax.random.uniform(ks[4], (C,), jnp.float32)
        mu_k = jax.random.uniform(ks[5], (C,), jnp.float32)
        return {'x': x, 'W_r': W_r, 'W_k': W_k, 'W_v': W_v, 'mu_r': mu_r, 'mu_k': mu_k}
    _L0_ffn_all = _L0_ffn_setup()
    _L0_ffn_in = {k: v for k, v in _L0_ffn_all.items() if k in ('W_r', 'W_k', 'W_v', 'mu_r', 'mu_k')}
    del _L0_ffn_all
    return {'x': x, 'ctx_2048': ctx_2048, 'mask_BxS2_if0': mask_BxS2_if0, 'L0_xattn_W_in': _L0_xattn_in['W_in'], 'L0_xattn_b_in': _L0_xattn_in['b_in'], 'L0_xattn_g_res': _L0_xattn_in['g_res'], 'L0_xattn_g_init': _L0_xattn_in['g_init'], 'L0_ffn_W_r': _L0_ffn_in['W_r'], 'L0_ffn_W_k': _L0_ffn_in['W_k'], 'L0_ffn_W_v': _L0_ffn_in['W_v'], 'L0_ffn_mu_r': _L0_ffn_in['mu_r'], 'L0_ffn_mu_k': _L0_ffn_in['mu_k']}

def reference(x, ctx_2048, mask_BxS2_if0, L0_xattn_W_in, L0_xattn_b_in, L0_xattn_g_res, L0_xattn_g_init, L0_ffn_W_r, L0_ffn_W_k, L0_ffn_W_v, L0_ffn_mu_r, L0_ffn_mu_k):
    import jax
    import jax.numpy as jnp

    def _L0_xattn_ref(embeds, patch_embeds, patch_lens, W_in, b_in, g_res, g_init):
        import jax, jax.numpy as jnp
        import numpy as np
        B, L, P = (4, 2048, 512)
        D_MODEL = 512
        D_GLOBAL = 1024
        HEADDIM = 32
        EPSILON = 0.001
        RMS_EPS = 1e-05

        def rmsnorm(x, g, eps=RMS_EPS):
            var = jnp.mean(jnp.square(x), axis=-1, keepdims=True)
            return x * jax.lax.rsqrt(var + eps) * g

        def _hnet_depool(h, h_patch_full, patch_lens):
            h_patch = h_patch_full[..., :D_MODEL]
            bsz, plen = (h_patch.shape[0], h_patch.shape[1])
            seqlen = h.shape[1]
            logp = jnp.full((bsz, plen), -EPSILON, dtype=jnp.float32)
            bidx = jnp.cumsum(patch_lens, axis=1) - 1
            boundary_mask = jnp.zeros((bsz, seqlen), dtype=jnp.int32)
            boundary_mask = boundary_mask.at[jnp.arange(bsz)[:, None], bidx].set(1)
            dt = (-jnp.log(-jnp.expm1(logp))).astype(h_patch.dtype)
            x = h_patch / dt[..., None]
            n_heads = D_MODEL // HEADDIM
            A = -jnp.ones((n_heads,), dtype=jnp.float32)
            bcoef = jnp.exp(logp).astype(h_patch.dtype)
            x4 = x.reshape(bsz, plen, n_heads, HEADDIM)
            a = jnp.exp(dt[:, :, None] * A[None, None, :])
            u = (dt * bcoef)[:, :, None, None] * x4
            a_b = jnp.broadcast_to(a[..., None], u.shape)

            def comb(lft, rgt):
                aL, uL = lft
                aR, uR = rgt
                return (aL * aR, uL * aR + uR)
            _, s = jax.lax.associative_scan(comb, (a_b, u), axis=1)
            depool = s.reshape(bsz, plen, D_MODEL)
            plug = jnp.clip(jnp.cumsum(boundary_mask, axis=1) - 1, 0, plen - 1)
            depool_out = depool[jnp.arange(bsz)[:, None], plug]
            return depool_out + h
        h = rmsnorm(embeds, g_res)
        h = jnp.einsum('bld,ed->ble', h, W_in) + b_in
        h_patch = rmsnorm(patch_embeds, g_init)
        return _hnet_depool(h, h_patch, patch_lens)

    def _L0_ffn_ref(x, W_r, W_k, W_v, mu_r, mu_k):
        import jax, jax.numpy as jnp
        import numpy as np
        DIM = 512

        def _reference_tuple_inner(x, W_r, W_k, W_v, mu_r, mu_k):
            B, T, C = x.shape
            x_prev = jnp.concatenate([jnp.zeros((B, 1, C), x.dtype), x[:, :-1, :]], axis=1)
            xr = mu_r * x + (1.0 - mu_r) * x_prev
            xk = mu_k * x + (1.0 - mu_k) * x_prev
            r = jax.nn.sigmoid(jnp.einsum('btc,dc->btd', xr, W_r))
            k = jnp.einsum('btc,dc->btd', xk, W_k)
            k_act = jnp.square(jax.nn.relu(k))
            out = r * jnp.einsum('btc,dc->btd', k_act, W_v)
            new_state = x[:, -1, :]
            return (out, new_state)
        return _reference_tuple_inner(x, W_r, W_k, W_v, mu_r, mu_k)[0]
    x = x + _L0_xattn_ref(_layernorm(x, axis=-1), ctx_2048, mask_BxS2_if0, L0_xattn_W_in, L0_xattn_b_in, L0_xattn_g_res, L0_xattn_g_init)
    x = x + _L0_ffn_ref(_layernorm(x, axis=-1), L0_ffn_W_r, L0_ffn_W_k, L0_ffn_W_v, L0_ffn_mu_r, L0_ffn_mu_k)
    return x

_drawn_inputs = setup_inputs


def setup_inputs(seed=0):
    import zlib

    import numpy as np

    out = dict(_drawn_inputs(seed))
    spreads = {'L0_xattn_b_in': (0.0, 0.1), 'L0_xattn_g_res': (1.0, 0.2), 'L0_xattn_g_init': (1.0, 0.2)}
    factors = {'L0_ffn_W_r': 3.705, 'L0_ffn_mu_r': 8.0}
    for name, (base, spread) in spreads.items():
        noise = np.random.default_rng([zlib.crc32(name.encode()), seed]).standard_normal(out[name].shape)
        drawn = base * np.exp(spread * noise) if base else spread * noise
        out[name] = jnp.asarray(drawn.astype(out[name].dtype))
    for name, factor in factors.items():
        out[name] = (out[name] * factor).astype(out[name].dtype)
    return out
```

```python
import math
from contextlib import ExitStack

import numpy as np

import concourse.bass as bass
from concourse import mybir

F32 = mybir.dt.float32
F32R = mybir.dt.float32r
BF16 = mybir.dt.bfloat16
I32 = mybir.dt.int32
ALU = mybir.AluOpType
ACT = mybir.ActivationFunctionType

P = 128
LN_EPS = 1e-5
RMS_EPS = 1e-5
EPSILON = 0.001
RING = 3


class Batch:

    def __init__(self, q, off):
        self.q, self.off = q + off // RING if isinstance(q, int) else q, off
        if isinstance(q, int):
            self.off = off % RING
        self.fixed = isinstance(q, int)
        self.slot = off % RING

    def number(self):
        return self.q * RING + self.off

    def plus(self, n):
        return Batch(self.q, self.off + n)

    def round(self):
        return self.q + self.off // RING

    def exists(self, count):
        return not self.fixed or 0 <= self.number() < count


def reached(eng, semaphore, batch, per_batch, done):
    value = batch.number() * per_batch + done
    if isinstance(value, int) and value <= 0:
        return
    eng.wait_ge(semaphore, value)


def hold(eng, passed):
    eng.sem_inc(passed, 1)


def batches(eng, iteration, count):
    rounds = (count - 4) // RING
    for n in range(-2, 1):
        iteration(Batch(0, n))
    with eng.Fori(0, rounds) as q:
        for off in range(1, RING + 1):
            iteration(Batch(q, off))
    for n in range(rounds * RING + 1, count):
        iteration(Batch(0, n))


def decay_powers():
    one = np.float32(1.0)
    dt = np.float32(-math.log(-math.expm1(float(np.float32(-EPSILON)))))
    a = np.float32(math.exp(-float(dt)))
    powers = [one]
    while powers[-1] * a > np.finfo(np.float32).tiny:
        powers.append(powers[-1] * a)
    return [float(p) for p in powers]


def build(nc, x, ctx, patch_lens, w_in, b_in, g_res, g_init, w_r, w_k, w_v, mu_r, mu_k, out):
    B, S, D = x.shape
    DG = ctx.shape[2]
    C = D // P
    T = S // P
    H16, W32 = 16, 32
    assert D == 512 and S == 512 and DG == 2 * D and B == 16 and H16 * W32 == S
    powers = decay_powers()
    input_gain = math.exp(-EPSILON)

    with ExitStack() as stack:
        def sb(name, shape, dt=F32):
            return stack.enter_context(nc.sbuf_tensor(name, shape, dt))

        def sem(name):
            return stack.enter_context(nc.semaphore(name))

        bank = [stack.enter_context(nc.psum_tensor(f"bank{i}", [P, 512], F32)) for i in range(8)]

        mask_rows = nc.dram_tensor("mask_rows", [B, S], F32, kind="Internal").ap()
        plug_rows = nc.dram_tensor("plug_rows", [B, S], F32, kind="Internal").ap()

        wt_hi = [sb(f"w{n}_hi", [P, C, D], F32R) for n in "irkv"]
        wt_lo = [sb(f"w{n}_lo", [P, C, D], F32R) for n in "irkv"]
        WIN, WR, WK, WV = range(4)
        ring = [sb(f"ring{i}", [P, T, D]) for i in range(RING)]
        turned = sb("turned", [P, C, S + 1])
        normed = sb("normed", [P, T, D])
        xt_hi, xt_lo = sb("xt_hi", [P, C, S], F32R), sb("xt_lo", [P, C, S], F32R)
        xk_hi, xk_lo = sb("xk_hi", [P, C, S], F32R), sb("xk_lo", [P, C, S], F32R)
        xr_hi, xr_lo = sb("xr_hi", [P, C, S], F32R), sb("xr_lo", [P, C, S], F32R)
        ka_hi, ka_lo = xr_hi, xr_lo
        gate = sb("gate", [P, T, D])
        scratch = sb("scratch", [P, 4, S])
        ctx_rows = sb("ctx_rows", [P, DG])
        u = sb("u", [P, D])
        u_hi, u_lo = sb("u_hi", [P, D], F32R), sb("u_lo", [P, D], F32R)
        s_hi, s_lo = sb("s_hi", [P, D], F32R), sb("s_lo", [P, D], F32R)
        hot = sb("hot", [P, S], F32R)
        far_hi, far_lo = sb("far_hi", [P, D], F32R), sb("far_lo", [P, D], F32R)
        far_hot = sb("far_hot", [P, S], F32R)
        plug = sb("plug", [P, S])
        bias = sb("bias", [P, D])
        g_ctx = sb("g_ctx", [P, D])
        g_rows = sb("g_rows", [P, D])
        ident = sb("ident", [P, P])
        decay = sb("decay", [P, 2, P])
        decay_hi, decay_lo = sb("decay_hi", [P, 2, P], F32R), sb("decay_lo", [P, 2, P], F32R)
        mus = sb("mus", [P, 4, C])
        part_i, part = sb("part_i", [P, 1], I32), sb("part", [P, 1])
        count_i = sb("count_i", [P, W32], I32)
        half = sb("half", [P, T])
        bn_a, mv_a, v_a, rs_a = (sb(f"{n}_a", [P, T, k]) for n, k in (("bn", 6), ("mv", 2), ("v", 1), ("rs", 1)))
        bn_b, mv_b, v_b, rs_b = (sb(f"{n}_b", [P, T, k]) for n, k in (("bn", 6), ("mv", 2), ("v", 1), ("rs", 1)))
        bn_c, mv_c, v_c, rs_c = (sb(f"{n}_c", [P, k]) for n, k in (("bn", 12), ("mv", 2), ("v", 2), ("rs", 1)))
        far_table = sb("far_table", [1, 2 * B], I32)
        far_f = sb("far_f", [1, 4, B])
        index_i = sb("index_i", [P, 3, T * B], I32)
        ones = sb("ones", [H16, S])

        lens = [u[0:B, :].bitcast(I32), plug[0:B, :].bitcast(I32)]
        index_f = u[0:B, :]
        low_hot = ring[1][:, 0:2, :].rearrange("p a b -> p (a b)").bitcast(BF16).rearrange("p (n w) -> p n w", w=W32)
        high_hot = ring[1][:, 2, :].bitcast(BF16).rearrange("p (n h) -> p n h", h=H16)
        staged = [gate, ring[2], scratch, normed]

        lens_loaded, rows_loaded, mus_loaded, g_loaded = (sem(n) for n in ("lens_loaded", "rows_loaded", "mus_loaded", "g_loaded"))
        w_loaded = [sem(f"w_loaded{i}") for i in range(4)]
        x_loaded = [sem(f"x_loaded{i}") for i in range(RING)]
        ctx_loaded, plug_loaded = sem("ctx_loaded"), sem("plug_loaded")
        ident_ready, decay_ready, decay_hi_ready, decay_lo_ready = (sem(n) for n in ("ident_ready", "decay_ready", "decay_hi_ready", "decay_lo_ready"))
        counts_ready, half_ready, zero_ready, g_ready, mus_ready, part_ready, g_applied = (
            sem(n) for n in ("counts_ready", "half_ready", "zero_ready", "g_ready", "mus_ready", "part_ready", "g_applied"))
        plug_step, index_turned, hots_ready, mask_counted, mask_copied, mask_stored, mask_loaded = (
            sem(n) for n in ("plug_step", "index_turned", "hots_ready", "mask_counted", "mask_copied", "mask_stored", "mask_loaded"))
        plug_made, plug_stored, last_loaded, table_ready = (sem(n) for n in ("plug_made", "plug_stored", "last_loaded", "table_ready"))
        w_turned, w_hi_ready, w_lo_ready = (sem(n) for n in ("w_turned", "w_hi_ready", "w_lo_ready"))
        bn_a_done, mv_a_done, v_a_done, rs_a_done, xn_ready, xb_ready = (
            sem(n) for n in ("bn_a_done", "mv_a_done", "v_a_done", "rs_a_done", "xn_ready", "xb_ready"))
        xn_turned, xt_hi_ready, xt_lo_ready, proj_done, x2_ready = (
            sem(n) for n in ("xn_turned", "xt_hi_ready", "xt_lo_ready", "proj_done", "x2_ready"))
        bn_c_done, mv_c_done, ms_c_done, v_c_done, rs_c_done = (sem(n) for n in ("bn_c_done", "mv_c_done", "ms_c_done", "v_c_done", "rs_c_done"))
        u_ready, u_hi_ready, u_lo_ready, s_done, s_hi_ready, s_lo_ready, hot_ready = (
            sem(n) for n in ("u_ready", "u_hi_ready", "u_lo_ready", "s_done", "s_hi_ready", "s_lo_ready", "hot_ready"))
        far_loaded, far_bn, far_mv, far_ms, far_v, far_rs, far_u, far_u_hi, far_u_lo = (
            sem(n) for n in ("far_loaded", "far_bn", "far_mv", "far_ms", "far_v", "far_rs", "far_u", "far_u_hi", "far_u_lo"))
        far_carried, far_s, far_s_hi, far_s_lo, far_hot_ready, far_picked, far_added = (
            sem(n) for n in ("far_carried", "far_s", "far_s_hi", "far_s_lo", "far_hot_ready", "far_picked", "far_added"))
        bn_b_done, mv_b_done, v_b_done, rs_b_done, yn_ready, yn_turned, yt_ready = (
            sem(n) for n in ("bn_b_done", "mv_b_done", "v_b_done", "rs_b_done", "yn_ready", "yn_turned", "yt_ready"))
        carried, mixed, mix_hi_ready, mix_lo_ready = (sem(n) for n in ("carried", "mixed", "mix_hi_ready", "mix_lo_ready"))
        r_done, gate_ready, k_done, relu_ready, square_ready, ka_hi_ready, ka_lo_ready = (
            sem(n) for n in ("r_done", "gate_ready", "k_done", "relu_ready", "square_ready", "ka_hi_ready", "ka_lo_ready"))
        dve_passed, pool_passed = sem("dve_passed"), sem("pool_passed")
        v_done, gated, out_ready = (sem(n) for n in ("v_done", "gated", "out_ready"))
        stored = [sem(f"stored{t}") for t in range(T)]

        def f32(ap):
            return ap.bitcast(F32)

        def tile(t):
            return slice(t * P, (t + 1) * P)

        x_rows = x.rearrange("b (t p) d -> b p t d", p=P)
        out_rows = out.rearrange("b (t p) d -> b p t d", p=P)

        def w_rows(w):
            return w.rearrange("(m p) c -> p m c", p=P)

        def far_count(eng, b):
            n = b.number()
            return (eng.value_load(far_table[0:1, bass.ds(n, 1)], min_val=0, max_val=1),
                    eng.value_load(far_table[0:1, bass.ds(n + B, 1)], min_val=0, max_val=B - 1))

        SHIFTS = [1 << k for k in range(S.bit_length() - 1)]
        INDEX_STEP = 2 * len(SHIFTS) + 4

        block = stack.enter_context(nc.Block())

        @block.sync
        def _(sp):
            sp.dma_start(lens[0], patch_lens).then_inc(lens_loaded, 16)
            sp.dma_start(g_rows[:, :], g_res.partition_broadcast(P)).then_inc(g_loaded, 16)
            sp.dma_start(staged[WIN][:, :, :], w_rows(w_in)).then_inc(w_loaded[WIN], 16)
            sp.dma_start(ring[0][:, :, :], x_rows[0]).then_inc(x_loaded[0], 16)
            sp.dma_start(bias[:, :], b_in.partition_broadcast(P)).then_inc(rows_loaded, 16)
            sp.dma_start(g_ctx[:, :], g_init[0:D].partition_broadcast(P)).then_inc(rows_loaded, 16)
            for n, mu in enumerate((mu_r, mu_k)):
                sp.dma_start(mus[:, n, :], mu.rearrange("(c p) -> p c", p=P),
                             allow_slow_non_contiguous=True).then_inc(mus_loaded, 16)
            sp.dma_start(ctx_rows[:, :], ctx[0, 0:P, :]).then_inc(ctx_loaded, 16)
            sp.dma_start(staged[WR][:, :, :], w_rows(w_r)).then_inc(w_loaded[WR], 16)
            sp.dma_start(staged[WK][:, :, :], w_rows(w_k)).then_inc(w_loaded[WK], 16)
            sp.dma_start(staged[WV][:, :, :], w_rows(w_v)).then_inc(w_loaded[WV], 16)
            sp.wait_ge(mask_copied, 1)
            sp.dma_start(mask_rows.rearrange("b (h w) -> h b w", w=W32),
                         u[0:H16, :].rearrange("h (b w) -> h b w", w=W32)).then_inc(mask_stored, 16)
            sp.dma_start(ring[1][:, :, :], x_rows[1]).then_inc(x_loaded[1], 16)
            sp.wait_ge(mask_stored, 16)
            sp.dma_start(plug[0:B, :], mask_rows).then_inc(mask_loaded, 16)
            sp.wait_ge(plug_made, 1)
            sp.dma_start(plug_rows, plug[0:B, :]).then_inc(plug_stored, 16)
            sp.wait_ge(plug_stored, 16)
            sp.dma_start(far_f[0:1, 0, :], plug_rows[:, S - 1:S].rearrange("b a -> a b"),
                         allow_slow_non_contiguous=True).then_inc(last_loaded, 16)

            def iteration(b):
                new = b.plus(2)
                if new.exists(B):
                    if not (new.fixed and new.number() < 2):
                        reached(sp, out_ready, b.plus(-1), T, T)
                        if new.fixed and new.number() == 2:
                            sp.wait_ge(w_turned, 2 * C)
                        sp.dma_start(ring[new.slot][:, :, :], x_rows[new.number()]).then_inc(x_loaded[new.slot], 16)
                    reached(sp, hot_ready, new.plus(-1), 1, 1)
                    if not (new.fixed and new.number() == 0):
                        sp.dma_start(ctx_rows[:, :], ctx[new.number(), 0:P, :]).then_inc(ctx_loaded, 16)
                    sp.dma_start(plug[:, :], plug_rows[new.number(), :].partition_broadcast(P)).then_inc(plug_loaded, 16)
                if b.exists(B):
                    for t in range(T):
                        reached(sp, out_ready, b, T, t + 1)
                        sp.dma_start(out_rows[b.number(), :, t, :], gate[:, t, :]).then_inc(stored[t], 16)

            batches(sp, iteration, B)
            for t in range(T):
                sp.wait_ge(stored[t], 16 * B)

        @block.gpsimd
        def _(pool):
            nc.gpsimd.memset(half[:, :], -0.5).then_inc(half_ready, 1)
            nc.gpsimd.memset(ident[:, :], 0.0).then_inc(ident_ready, 1)
            pool.wait_ge(ident_ready, 1)
            nc.gpsimd.affine_select(out=ident[:, :], in_=ident[:, :], compare_op=ALU.not_equal, fill=1.0, base=0,
                                    pattern=[[-1, P]], channel_multiplier=1).then_inc(ident_ready, 1)
            nc.gpsimd.iota(count_i[:, :], pattern=[[1, W32]], base=0, channel_multiplier=0).then_inc(counts_ready, 1)
            nc.gpsimd.iota(part_i[:, :], pattern=[[1, 1]], base=0, channel_multiplier=1).then_inc(counts_ready, 1)
            nc.gpsimd.memset(ones[:, :], 1.0).then_inc(counts_ready, 1)
            def make_decay():
                nc.gpsimd.memset(decay[:, :, :], 0.0).then_inc(decay_ready, 1)
                steps = 1
                for which, base in ((0, 0), (1, P)):
                    for k, value in enumerate(powers):
                        if which == 1 and k == 0:
                            continue
                        pool.wait_ge(decay_ready, steps)
                        nc.gpsimd.affine_select(out=decay[:, which, :], in_=decay[:, which, :], compare_op=ALU.not_equal,
                                                fill=value, base=base - k, pattern=[[1, P]],
                                                channel_multiplier=-1).then_inc(decay_ready, 1)
                        steps += 1

            def far(b):
                n = far_count(pool, b)
                with pool.If(n[0] > 0):
                    for c in range(1, T):
                        done = n[1] * (T - 1) + c
                        if c == 1:
                            reached(pool, u_ready, b, 1, 1)
                        else:
                            pool.wait_ge(far_u, done - 1)
                        hold(pool, pool_passed)
                        pool.dma_start(ctx_rows[:, :], ctx[b.number(), c * P:(c + 1) * P, :]).then_inc(far_loaded, 16)
                        pool.wait_ge(far_v, done)
                        nc.gpsimd.tensor_tensor(rs_c[:, :], v_c[:, 1:2], half[:, 0:1], ALU.pow).then_inc(far_rs, 1)

            def iteration(b):
                nxt, new = b.plus(1), b.plus(2)
                if new.fixed and new.number() == 0:
                    pool.wait_ge(half_ready, 1)
                if nxt.exists(B):
                    reached(pool, v_b_done, nxt, 1, 1)
                    reached(pool, yn_ready, b, T, T)
                    nc.gpsimd.tensor_tensor(rs_b[:, :, 0], v_b[:, :, 0], half[:, :], ALU.pow).then_inc(rs_b_done, 1)
                if new.exists(B):
                    reached(pool, v_a_done, new, 1, 1)
                    nc.gpsimd.tensor_tensor(rs_a[:, :, 0], v_a[:, :, 0], half[:, :], ALU.pow).then_inc(rs_a_done, 1)
                    reached(pool, v_c_done, new, 1, 1)
                    reached(pool, u_ready, new.plus(-1), 1, 1)
                    nc.gpsimd.tensor_tensor(rs_c[:, :], v_c[:, 1:2], half[:, 0:1], ALU.pow).then_inc(rs_c_done, 1)
                    if new.fixed and new.number() == 0:
                        pool.wait_ge(rows_loaded, 32)
                    reached(pool, xn_ready, new, T, T)
                    nc.gpsimd.tensor_tensor(ring[new.slot][:, :, :], ring[new.slot][:, :, :],
                                            bias[:, :].unsqueeze(1).to_broadcast([P, T, D]), ALU.add).then_inc(xb_ready, 1)
                if b.exists(B):
                    for t in range(T):
                        reached(pool, gated, b, T, t + 1)
                        nc.gpsimd.tensor_tensor(gate[:, t, :], gate[:, t, :], ring[b.slot][:, t, :],
                                                ALU.add).then_inc(out_ready, 1)
                if new.exists(B):
                    if new.fixed and new.number() == 0:
                        make_decay()
                        pool.wait_ge(table_ready, 2)
                    far(new)

            batches(pool, iteration, B)

        @block.tensor
        def _(pe):
            def product(where, lhs_hi, lhs_lo, rhs_hi, rhs_lo, start, stop):
                nc.tensor.matmul(where, lhs_hi, rhs_hi, start=start, stop=False)
                nc.tensor.matmul(where, lhs_hi, rhs_lo, start=False, stop=False)
                return nc.tensor.matmul(where, lhs_lo, rhs_hi, start=False, stop=stop)

            def turn_weight(w):
                pe.wait_ge(w_loaded[w], 16)
                for c in range(C):
                    at = w * C + c
                    if at >= 4:
                        pe.wait_ge(w_lo_ready, at - 3)
                    for m in range(C):
                        last = nc.tensor.transpose(bank[4 + c][:, tile(m)], staged[w][:, m, tile(c)], ident[:, :])
                    last.then_inc(w_turned, 1)

            def turn(source, t, where):
                for c in range(C):
                    last = nc.tensor.transpose(bank[where][:, tile(c)], source[:, t, c * P:(c + 1) * P], ident[:, :])
                return last

            turned_rows = turned[:, :, 1:S + 1]

            pe.wait_ge(ident_ready, 2)
            pe.wait_ge(g_applied, 1)
            turn_weight(WIN)

            def project(b):
                for t in range(T):
                    reached(pe, xt_lo_ready, b, T, t + 1)
                    reached(pe, gated, b.plus(-2), T, t + 1)
                    for c in range(C):
                        product(bank[t][:, :], xt_hi[:, c, tile(t)], xt_lo[:, c, tile(t)],
                                wt_hi[WIN][:, c, :], wt_lo[WIN][:, c, :], c == 0, False)
                    if t == 0:
                        reached(pe, hot_ready, b, 1, 1)
                        reached(pe, s_lo_ready, b, 1, 1)
                    nc.tensor.matmul(bank[t][:, :], hot[:, tile(t)], s_hi[:, :], start=False, stop=False)
                    nc.tensor.matmul(bank[t][:, :], hot[:, tile(t)], s_lo[:, :], start=False, stop=True).then_inc(proj_done, 1)

            def far(b):
                n = far_count(pe, b)
                with pe.If(n[0] > 0):
                    for c in range(1, T):
                        done = n[1] * (T - 1) + c
                        if c > 1:
                            pe.wait_ge(far_added, (done - 1) * T)
                        else:
                            reached(pe, s_lo_ready, b, 1, 1)
                        product(bank[4][:, :], decay_hi[:, 1, :], decay_lo[:, 1, :], u_hi[:, :], u_lo[:, :],
                                True, False).then_inc(far_carried, 1)
                        pe.wait_ge(far_u_lo, done)
                        product(bank[4][:, :], decay_hi[:, 0, :], decay_lo[:, 0, :], u_hi[:, :], u_lo[:, :],
                                False, True).then_inc(far_s, 1)
                        pe.wait_ge(far_s_lo, done)
                        pe.wait_ge(far_hot_ready, done)
                        for t in range(T):
                            if t:
                                pe.wait_ge(far_added, (done - 1) * T + t)
                            nc.tensor.matmul(bank[4][:, :], far_hot[:, tile(t)], far_hi[:, :], start=True, stop=False)
                            nc.tensor.matmul(bank[4][:, :], far_hot[:, tile(t)], far_lo[:, :], start=False,
                                             stop=True).then_inc(far_picked, 1)

            def pick_tokens():
                pe.wait_ge(plug_step, INDEX_STEP)
                for j in range(T):
                    last = nc.tensor.transpose(bank[1][:, j * B:(j + 1) * B], index_f[:, tile(j)], ident[0:B, 0:B])
                last.then_inc(index_turned, 1)
                pe.wait_ge(hots_ready, 2)
                for n in range(B):
                    for j in range(T):
                        last = nc.tensor.matmul(bank[0][0:H16, n * W32:(n + 1) * W32], high_hot[:, j * B + n, :],
                                                low_hot[:, j * B + n, :], start=j == 0, stop=j == T - 1)
                last.then_inc(mask_counted, 1)

            def iteration(b):
                nxt, new = b.plus(1), b.plus(2)
                if nxt.exists(B):
                    if nxt.fixed and nxt.number() == 0:
                        pe.wait_ge(mask_copied, 1)
                    project(nxt)
                if b.exists(B):
                    for t in range(T):
                        reached(pe, yt_ready, b, T, T)
                        reached(pe, mix_lo_ready, b, 2 * C, C)
                        for c in range(C):
                            last = product(bank[4 + t][:, :], xr_hi[:, c, tile(t)], xr_lo[:, c, tile(t)],
                                           wt_hi[WR][:, c, :], wt_lo[WR][:, c, :], c == 0, c == C - 1)
                        last.then_inc(r_done, 1)
                    for m in range(C):
                        reached(pe, mix_lo_ready, b, 2 * C, 2 * C)
                        if nxt.exists(B):
                            reached(pe, x2_ready, nxt, T, m + 1)
                        else:
                            reached(pe, gated, b.plus(-1), T, m + 1)
                        for c in range(C):
                            last = product(bank[m][:, :], wt_hi[WK][:, c, tile(m)], wt_lo[WK][:, c, tile(m)],
                                           xk_hi[:, c, :], xk_lo[:, c, :], c == 0, c == C - 1)
                        last.then_inc(k_done, 1)
                if new.exists(B):
                    for t in range(T):
                        reached(pe, xn_ready, new, T, t + 1)
                        if b.exists(B):
                            reached(pe, gate_ready, b, T, t + 1)
                        elif new.fixed and new.number() == 0:
                            pe.wait_ge(w_lo_ready, t + 1)
                        else:
                            pe.wait_ge(w_lo_ready, 4 * C)
                            reached(pe, s_lo_ready, new.plus(-1), 1, 1)
                        turn(turned_rows, t, 4 + t).then_inc(xn_turned, 1)
                if b.exists(B):
                    for t in range(T):
                        if t == 0:
                            reached(pe, relu_ready, b, C, C)
                        for m in range(C):
                            if t == 0:
                                reached(pe, ka_lo_ready, b, C, m + 1)
                            last = product(bank[t][:, :], ka_hi[:, m, tile(t)], ka_lo[:, m, tile(t)],
                                           wt_hi[WV][:, m, :], wt_lo[WV][:, m, :], m == 0, m == C - 1)
                        last.then_inc(v_done, 1)
                if new.fixed and new.number() == 0:
                    pick_tokens()
                    reached(pe, xt_lo_ready, new, T, T)
                    for w in (WR, WK, WV):
                        turn_weight(w)
                    pe.wait_ge(w_lo_ready, 4 * C)
                if new.exists(B):
                    reached(pe, xt_lo_ready, new, T, 1)
                    reached(pe, u_lo_ready, new, 1, 1)
                    if new.fixed and new.number() == 0:
                        pe.wait_ge(decay_lo_ready, 1)
                    product(bank[4][:, :], decay_hi[:, 0, :], decay_lo[:, 0, :], u_hi[:, :], u_lo[:, :],
                            True, True).then_inc(s_done, 1)
                    if new.fixed and new.number() == 0:
                        pe.wait_ge(table_ready, 2)
                    far(new)
                if nxt.exists(B):
                    for t in range(T):
                        reached(pe, yn_ready, nxt, T, t + 1)
                        if new.exists(B):
                            reached(pe, xt_lo_ready, new, T, t + 2 if t < T - 1 else 1)
                            if t == T - 1:
                                reached(pe, hot_ready, new, 1, 1)
                        else:
                            reached(pe, gate_ready, b, T, t + 2 if t < T - 1 else 1)
                        turn(normed, t, 4 + (t + 1) % T).then_inc(yn_turned, 1)

            batches(pe, iteration, B)

        @block.scalar
        def _(act):
            def copy(to, of):
                return nc.scalar.activation(to, of, ACT.Copy)

            def weight_hi(w):
                for c in range(C):
                    act.wait_ge(w_turned, w * C + c + 1)
                    copy(wt_hi[w][:, c, :], bank[4 + c][:, :]).then_inc(w_hi_ready, 1)

            weight_hi(WIN)

            def iteration(b):
                nxt, new = b.plus(1), b.plus(2)
                if b.exists(B):
                    for i in range(2 * C):
                        to = (xr_hi if i < C else xk_hi)[:, i % C, :]
                        reached(act, mixed, b, 2 * C, i + 1)
                        if i == 0:
                            reached(act, v_done, b.plus(-1), T, T)
                        copy(to, scratch[:, 2 + i % 2, :]).then_inc(mix_hi_ready, 1)
                    for t in range(T):
                        reached(act, r_done, b, T, t + 1)
                        reached(act, stored[t], b, 16, 0)
                        nc.scalar.activation(gate[:, t, :], bank[4 + t][:, :], ACT.Sigmoid).then_inc(gate_ready, 1)
                    for m in range(C):
                        reached(act, k_done, b, C, m + 1)
                        if m == 0:
                            reached(act, mix_lo_ready, b, 2 * C, 2 * C)
                        if m >= 2:
                            reached(act, ka_lo_ready, b, C, m - 1)
                        nc.scalar.activation(scratch[:, m % 2, :], bank[m][:, :], ACT.Relu).then_inc(relu_ready, 1)
                        reached(act, relu_ready, b, C, m + 1)
                        nc.scalar.activation(scratch[:, 2 + m % 2, :], scratch[:, m % 2, :], ACT.Square).then_inc(square_ready, 1)
                        reached(act, square_ready, b, C, m + 1)
                        copy(ka_hi[:, m, :], scratch[:, 2 + m % 2, :]).then_inc(ka_hi_ready, 1)
                if new.exists(B):
                    for t in range(T):
                        reached(act, xn_turned, new, T, t + 1)
                        if t == 0:
                            reached(act, proj_done, nxt, T, T)
                        copy(xt_hi[:, :, tile(t)], bank[4 + t][:, :].rearrange("p (c n) -> p c n", c=C)).then_inc(xt_hi_ready, 1)
                    if new.fixed and new.number() == 0:
                        for w in (WR, WK, WV):
                            weight_hi(w)
                        act.wait_ge(decay_ready, 2 * len(powers))
                        copy(decay_hi[:, :, :], decay[:, :, :]).then_inc(decay_hi_ready, 1)
                    reached(act, u_ready, new, 1, 1)
                    reached(act, hot_ready, new.plus(-1), 1, 1)
                    copy(u_hi[:, :], u[:, :]).then_inc(u_hi_ready, 1)
                    reached(act, s_done, new, 1, 1)
                    copy(s_hi[:, :], bank[4][:, :]).then_inc(s_hi_ready, 1)
                if nxt.exists(B):
                    for t in range(T):
                        reached(act, yn_turned, nxt, T, t + 1)
                        if t == 0:
                            reached(act, mix_lo_ready, b, 2 * C, 2 * C)
                        copy(turned[:, :, 1 + t * P:1 + (t + 1) * P],
                             bank[4 + (t + 1) % T][:, :].rearrange("p (c n) -> p c n", c=C)).then_inc(yt_ready, 1)

            batches(act, iteration, B)

        @block.vector
        def _(dve):
            steps = [0]

            def step(instruction):
                instruction.then_inc(plug_step, 1)
                steps[0] += 1
                dve.wait_ge(plug_step, steps[0])

            def low(to, whole, high):
                return nc.vector.tensor_tensor(to, whole, high, ALU.subtract)

            def weight_lo(w):
                for c in range(C):
                    dve.wait_ge(w_hi_ready, w * C + c + 1)
                    low(wt_lo[w][:, c, :], bank[4 + c][:, :], f32(wt_hi[w][:, c, :])).then_inc(w_lo_ready, 1)

            def stats_a(new):
                dve.wait_ge(x_loaded[new.slot], (new.round() + 1) * 16)
                for t in range(T):
                    nc.vector.bn_stats(bn_a[:, t, :], ring[new.slot][:, t, :]).then_inc(bn_a_done, 1)
                reached(dve, bn_a_done, new, T, T)
                hold(dve, dve_passed)
                for t in range(T):
                    nc.vector.bn_aggr(mv_a[:, t, :], bn_a[:, t, :]).then_inc(mv_a_done, 1)
                reached(dve, mv_a_done, new, T, T)
                nc.vector.tensor_scalar(v_a[:, :, 0], mv_a[:, :, 1], 1.0 + RMS_EPS, RMS_EPS * LN_EPS,
                                        ALU.mult, ALU.add).then_inc(v_a_done, 1)

            def norm_a(new):
                reached(dve, rs_a_done, new, 1, 1)
                reached(dve, mix_lo_ready, new.plus(-2), 2 * C, 2 * C)
                for t in range(T):
                    nc.vector.tensor_scalar(turned[:, t, 1:S + 1], ring[new.slot][:, t, :], mv_a[:, t, 0:1], rs_a[:, t, :],
                                            ALU.subtract, ALU.mult).then_inc(xn_ready, 1)

            def stats_c(new):
                reached(dve, ctx_loaded, new, 16, 16)
                for h in range(2):
                    nc.vector.bn_stats(bn_c[:, 6 * h:6 * h + 6], ctx_rows[:, h * D:(h + 1) * D]).then_inc(bn_c_done, 1)
                reached(dve, bn_c_done, new, 2, 2)
                hold(dve, dve_passed)
                nc.vector.bn_aggr(mv_c[:, :], bn_c[:, :]).then_inc(mv_c_done, 1)
                reached(dve, mv_c_done, new, 1, 1)
                nc.vector.scalar_tensor_tensor(v_c[:, 0:1], mv_c[:, 0:1], mv_c[:, 0:1], mv_c[:, 1:2],
                                               ALU.mult, ALU.add).then_inc(ms_c_done, 1)
                reached(dve, ms_c_done, new, 1, 1)
                nc.vector.tensor_scalar(v_c[:, 1:2], v_c[:, 0:1], RMS_EPS, None, ALU.add).then_inc(v_c_done, 1)

            def scan_input(new):
                reached(dve, rs_c_done, new, 1, 1)
                reached(dve, u_lo_ready, new.plus(-1), 1, 1)
                nc.vector.scalar_tensor_tensor(u[:, :], ctx_rows[:, 0:D], rs_c[:, :], g_ctx[:, :],
                                               ALU.mult, ALU.mult).then_inc(u_ready, 1)

            def far(b):
                n = far_count(dve, b)
                with dve.If(n[0] > 0):
                    reached(dve, xb_ready, b, 1, 1)
                    reached(dve, plug_loaded, b, 16, 16)
                    for c in range(1, T):
                        done = n[1] * (T - 1) + c
                        dve.wait_ge(far_loaded, done * 16)
                        for h in range(2):
                            nc.vector.bn_stats(bn_c[:, 6 * h:6 * h + 6], ctx_rows[:, h * D:(h + 1) * D]).then_inc(far_bn, 1)
                        dve.wait_ge(far_bn, done * 2)
                        hold(dve, dve_passed)
                        nc.vector.bn_aggr(mv_c[:, :], bn_c[:, :]).then_inc(far_mv, 1)
                        dve.wait_ge(far_mv, done)
                        nc.vector.scalar_tensor_tensor(v_c[:, 0:1], mv_c[:, 0:1], mv_c[:, 0:1], mv_c[:, 1:2],
                                                       ALU.mult, ALU.add).then_inc(far_ms, 1)
                        dve.wait_ge(far_ms, done)
                        nc.vector.tensor_scalar(v_c[:, 1:2], v_c[:, 0:1], RMS_EPS, None, ALU.add).then_inc(far_v, 1)
                        dve.wait_ge(far_rs, done)
                        nc.vector.scalar_tensor_tensor(u[:, :], ctx_rows[:, 0:D], rs_c[:, :], g_ctx[:, :],
                                                       ALU.mult, ALU.mult).then_inc(far_u, 1)
                        dve.wait_ge(far_u, done)
                        dve.wait_ge(far_carried, done)
                        nc.vector.tensor_copy(u_hi[:, :], u[:, :]).then_inc(far_u_hi, 1)
                        dve.wait_ge(far_u_hi, done)
                        low(u_lo[:, :], u[:, :], f32(u_hi[:, :])).then_inc(far_u_lo, 1)
                        nc.vector.tensor_scalar(far_hot[:, :], plug[:, :], float(c * P), part[:, :],
                                                ALU.subtract, ALU.is_equal).then_inc(far_hot_ready, 1)
                        dve.wait_ge(far_s, done)
                        nc.vector.tensor_copy(far_hi[:, :], bank[4][:, :]).then_inc(far_s_hi, 1)
                        dve.wait_ge(far_s_hi, done)
                        low(far_lo[:, :], bank[4][:, :], f32(far_hi[:, :])).then_inc(far_s_lo, 1)
                        for t in range(T):
                            dve.wait_ge(far_picked, (done - 1) * T + t + 1)
                            if c > 1:
                                dve.wait_ge(far_added, (done - 2) * T + t + 1)
                            nc.vector.tensor_tensor(ring[b.slot][:, t, :], bank[4][:, :], ring[b.slot][:, t, :],
                                                    ALU.add).then_inc(far_added, 1)
                    dve.wait_ge(far_added, (n[1] * (T - 1) + T - 1) * T)
                    hold(dve, dve_passed)

            def carry(b, i):
                row = 2 + i // C
                nc.vector.tensor_scalar(scratch[:, i % 2, :], turned[:, i % C, 0:S], mus[:, row, i % C:i % C + 1], None,
                                        ALU.mult).then_inc(carried, 1)

            def mix(b, i):
                reached(dve, carried, b, 2 * C, i + 1)
                nc.vector.scalar_tensor_tensor(scratch[:, 2 + i % 2, :], turned[:, i % C, 1:S + 1],
                                               mus[:, i // C, i % C:i % C + 1], scratch[:, i % 2, :],
                                               ALU.mult, ALU.add).then_inc(mixed, 1)

            def mix_low(b, i):
                reached(dve, mix_hi_ready, b, 2 * C, i + 1)
                hi, lo = (xr_hi, xr_lo) if i < C else (xk_hi, xk_lo)
                low(lo[:, i % C, :], scratch[:, 2 + i % 2, :], f32(hi[:, i % C, :])).then_inc(mix_lo_ready, 1)

            def mixing(b, first, last):
                for i in range(first, last):
                    if i >= 1:
                        reached(dve, mixed, b, 2 * C, i)
                    if i == 0:
                        carry(b, 0)
                    if i + 1 < 2 * C:
                        carry(b, i + 1)
                    if i >= 2:
                        reached(dve, mix_lo_ready, b, 2 * C, i - 1)
                    mix(b, i)
                    if i >= 1:
                        mix_low(b, i - 1)
                if last == 2 * C:
                    mix_low(b, last - 1)

            def add_x(b, t):
                reached(dve, proj_done, b, T, t + 1)
                if t == 0:
                    reached(dve, xb_ready, b, 1, 1)
                nc.vector.tensor_tensor(ring[b.slot][:, t, :], bank[t][:, :], ring[b.slot][:, t, :], ALU.add).then_inc(x2_ready, 1)

            def stats_b(b):
                for t in range(T):
                    reached(dve, x2_ready, b, T, t + 1)
                    nc.vector.bn_stats(bn_b[:, t, :], ring[b.slot][:, t, :]).then_inc(bn_b_done, 1)
                reached(dve, bn_b_done, b, T, T)
                hold(dve, dve_passed)
                for t in range(T):
                    nc.vector.bn_aggr(mv_b[:, t, :], bn_b[:, t, :]).then_inc(mv_b_done, 1)
                reached(dve, mv_b_done, b, T, T)
                nc.vector.tensor_scalar(v_b[:, :, 0], mv_b[:, :, 1], LN_EPS, None, ALU.add).then_inc(v_b_done, 1)

            def norm_b(b):
                reached(dve, rs_b_done, b, 1, 1)
                reached(dve, yn_turned, b.plus(-1), T, T)
                for t in range(T):
                    nc.vector.tensor_scalar(normed[:, t, :], ring[b.slot][:, t, :], mv_b[:, t, 0:1], rs_b[:, t, :],
                                            ALU.subtract, ALU.mult).then_inc(yn_ready, 1)

            dve.wait_ge(lens_loaded, 16)
            here, there = lens
            for shift in SHIFTS:
                step(nc.vector.tensor_copy(there[:, 0:shift], here[:, 0:shift]))
                step(nc.vector.tensor_tensor(there[:, shift:S], here[:, shift:S], here[:, 0:S - shift], ALU.add))
                here, there = there, here
            total = here
            whole, spare = (plug[0:B, :], index_f) if total is lens[0] else (index_f, plug[0:B, :])
            step(nc.vector.tensor_scalar(whole, total, -1.0, None, ALU.add))
            step(nc.vector.tensor_scalar(spare, whole, 0.0, float(S), ALU.is_lt, ALU.mult))
            step(nc.vector.tensor_tensor(spare, whole, spare, ALU.add))
            step(nc.vector.tensor_scalar(index_f, spare, -1.0, float(2 * S - 1), ALU.max, ALU.min))
            assert steps[0] == INDEX_STEP

            dve.wait_ge(g_loaded, 16)
            dve.wait_ge(w_loaded[WIN], 16)
            nc.vector.tensor_tensor(staged[WIN][:, :, :], staged[WIN][:, :, :],
                                    g_rows[:, :].unsqueeze(1).to_broadcast([P, T, D]), ALU.mult).then_inc(g_applied, 1)
            nc.vector.memset(turned[:, :, 0:1], 0.0).then_inc(zero_ready, 1)
            stats_a(Batch(0, 0))
            norm_a(Batch(0, 0))
            dve.wait_ge(rows_loaded, 32)
            nc.vector.tensor_scalar(g_ctx[:, :], g_ctx[:, :], input_gain, None, ALU.mult).then_inc(g_ready, 1)
            dve.wait_ge(mus_loaded, 32)
            nc.vector.tensor_scalar(mus[:, 2:4, :], mus[:, 0:2, :], -1.0, 1.0, ALU.mult, ALU.add).then_inc(mus_ready, 1)
            dve.wait_ge(counts_ready, 3)
            nc.vector.tensor_copy(part[:, :], part_i[:, :]).then_inc(part_ready, 1)
            weight_lo(WIN)

            dve.wait_ge(index_turned, 1)
            step(nc.vector.tensor_copy(index_i[:, 0, :], bank[1][:, 0:T * B]))
            step(nc.vector.tensor_scalar(index_i[:, 1, :], index_i[:, 0, :], 5, None, ALU.arith_shift_right))
            step(nc.vector.tensor_scalar(index_i[:, 2, :], index_i[:, 0, :], W32 - 1, None, ALU.bitwise_and))
            nc.vector.tensor_tensor(high_hot, index_i[:, 1, :].unsqueeze(2).to_broadcast([P, T * B, H16]),
                                    count_i[:, 0:H16].unsqueeze(1).to_broadcast([P, T * B, H16]),
                                    ALU.is_equal).then_inc(hots_ready, 1)
            nc.vector.tensor_tensor(low_hot, index_i[:, 2, :].unsqueeze(2).to_broadcast([P, T * B, W32]),
                                    count_i[:, :].unsqueeze(1).to_broadcast([P, T * B, W32]),
                                    ALU.is_equal).then_inc(hots_ready, 1)

            def plug_table():
                dve.wait_ge(mask_loaded, 16)
                step(nc.vector.tensor_tensor_scan(u[0:B, :], ones[:, :], plug[0:B, :], 0.0, ALU.mult, ALU.add))
                nc.vector.tensor_scalar(plug[0:B, :], u[0:B, :], -1.0, 0.0, ALU.add, ALU.max).then_inc(plug_made, 1)
                dve.wait_ge(last_loaded, 16)
                step(nc.vector.tensor_scalar(far_f[:, 1, :], far_f[:, 0, :], float(P), None, ALU.is_ge))
                step(nc.vector.tensor_tensor_scan(far_f[:, 2, :], ones[0:1, 0:B], far_f[:, 1, :], 0.0, ALU.mult, ALU.add))
                step(nc.vector.tensor_tensor(far_f[:, 3, :], far_f[:, 2, :], far_f[:, 1, :], ALU.subtract))
                nc.vector.tensor_copy(far_table[:, 0:B], far_f[:, 1, :]).then_inc(table_ready, 1)
                nc.vector.tensor_copy(far_table[:, B:2 * B], far_f[:, 3, :]).then_inc(table_ready, 1)
                dve.wait_ge(table_ready, 2)

            def iteration(b):
                nxt, new = b.plus(1), b.plus(2)
                setup = new.fixed and new.number() == 0
                if b.exists(B):
                    if b.fixed and b.number() == 0:
                        dve.wait_ge(mus_ready, 1)
                        dve.wait_ge(zero_ready, 1)
                        dve.wait_ge(w_turned, (WK + 1) * C)
                    reached(dve, yt_ready, b, T, T)
                    reached(dve, v_done, b.plus(-1), T, T)
                    mixing(b, 0, C + 1)
                if nxt.exists(B):
                    add_x(nxt, 0)
                    add_x(nxt, 1)
                if b.exists(B):
                    mixing(b, C + 1, 2 * C - 1)
                if nxt.exists(B):
                    add_x(nxt, 2)
                if b.exists(B):
                    mixing(b, 2 * C - 1, 2 * C)
                if nxt.exists(B):
                    add_x(nxt, 3)
                    stats_b(nxt)
                if new.exists(B):
                    if not setup:
                        stats_a(new)
                    stats_c(new)
                if nxt.exists(B):
                    if nxt.fixed and nxt.number() == 0:
                        dve.wait_ge(w_turned, (WV + 1) * C)
                    norm_b(nxt)
                if new.exists(B):
                    if not setup:
                        norm_a(new)
                    else:
                        dve.wait_ge(g_ready, 1)
                        dve.wait_ge(mask_stored, 16)
                    if not setup:
                        scan_input(new)
                if b.exists(B):
                    for m in range(C):
                        reached(dve, ka_hi_ready, b, C, m + 1)
                        low(ka_lo[:, m, :], scratch[:, 2 + m % 2, :], f32(ka_hi[:, m, :])).then_inc(ka_lo_ready, 1)
                if new.exists(B):
                    for t in range(T):
                        reached(dve, xt_hi_ready, new, T, t + 1)
                        low(xt_lo[:, :, tile(t)], bank[4 + t][:, :].rearrange("p (c n) -> p c n", c=C),
                            f32(xt_hi[:, :, tile(t)])).then_inc(xt_lo_ready, 1)
                    if setup:
                        for w in (WR, WK, WV):
                            weight_lo(w)
                        plug_table()
                        scan_input(new)
                        dve.wait_ge(decay_hi_ready, 1)
                        low(decay_lo[:, :, :], decay[:, :, :], f32(decay_hi[:, :, :])).then_inc(decay_lo_ready, 1)
                    reached(dve, u_hi_ready, new, 1, 1)
                    low(u_lo[:, :], u[:, :], f32(u_hi[:, :])).then_inc(u_lo_ready, 1)
                if b.exists(B):
                    for t in range(T):
                        reached(dve, v_done, b, T, t + 1)
                        reached(dve, gate_ready, b, T, t + 1)
                        nc.vector.tensor_tensor(gate[:, t, :], bank[t][:, :], gate[:, t, :], ALU.mult).then_inc(gated, 1)
                if new.exists(B):
                    reached(dve, s_hi_ready, new, 1, 1)
                    low(s_lo[:, :], bank[4][:, :], f32(s_hi[:, :])).then_inc(s_lo_ready, 1)
                    if setup:
                        dve.wait_ge(part_ready, 1)
                    far(new)
                    reached(dve, plug_loaded, new, 16, 16)
                    nc.vector.tensor_scalar(hot[:, :], plug[:, :], part[:, :], None, ALU.is_equal).then_inc(hot_ready, 1)

            dve.wait_ge(mask_counted, 1)
            nc.vector.tensor_scalar(u[0:H16, :], bank[0][0:H16, :], 1.0, None, ALU.min).then_inc(mask_copied, 1)
            batches(dve, iteration, B)


_INS = ["x", "ctx_2048", "mask_BxS2_if0", "L0_xattn_W_in", "L0_xattn_b_in", "L0_xattn_g_res", "L0_xattn_g_init",
        "L0_ffn_W_r", "L0_ffn_W_k", "L0_ffn_W_v", "L0_ffn_mu_r", "L0_ffn_mu_k"]


def kernel(**inputs):
    import concourse.bacc as bacc
    from concourse.bass_utils import run_bass_kernel_spmd

    nc = bacc.Bacc("TRN2", target_bir_lowering=False, num_devices=1)
    arrays, args = {}, []
    for name in _INS:
        a = np.ascontiguousarray(inputs[name])
        arrays[f"in_{name}"] = a
        args.append(nc.dram_tensor(f"in_{name}", a.shape, mybir.dt.from_np(a.dtype), kind="ExternalInput").ap())
    shape = arrays["in_x"].shape
    args.append(nc.dram_tensor("out_0", shape, F32, kind="ExternalOutput").ap())
    build(nc, *args)
    r = run_bass_kernel_spmd(nc, [arrays], core_ids=[0])
    return r.results[0]["out_0"]
```

```python
import math
from contextlib import ExitStack

import numpy as np

import concourse.bass as bass
from concourse import mybir

F32 = mybir.dt.float32
F32R = mybir.dt.float32r
BF16 = mybir.dt.bfloat16
I32 = mybir.dt.int32
U32 = mybir.dt.uint32
ALU = mybir.AluOpType
ACT = mybir.ActivationFunctionType

P = 128
LN_EPS = 1e-5
RMS_EPS = 1e-5
EPSILON = 0.001
RING = 3


class Batch:

    def __init__(self, q, off):
        self.q, self.off = q + off // RING if isinstance(q, int) else q, off
        if isinstance(q, int):
            self.off = off % RING
        self.fixed = isinstance(q, int)
        self.slot = off % RING

    def number(self):
        return self.q * RING + self.off

    def plus(self, n):
        return Batch(self.q, self.off + n)

    def round(self):
        return self.q + self.off // RING

    def exists(self, count):
        return not self.fixed or 0 <= self.number() < count


def reached(eng, semaphore, batch, per_batch, done):
    value = batch.number() * per_batch + done
    if isinstance(value, int) and value <= 0:
        return
    eng.wait_ge(semaphore, value)


def hold(eng, passed):
    eng.sem_inc(passed, 1)


def batches(eng, iteration, count):
    rounds = (count - 4) // RING
    for n in range(-2, 1):
        iteration(Batch(0, n))
    with eng.Fori(0, rounds) as q:
        for off in range(1, RING + 1):
            iteration(Batch(q, off))
    for n in range(rounds * RING + 1, count):
        iteration(Batch(0, n))


def decay_powers():
    one = np.float32(1.0)
    dt = np.float32(-math.log(-math.expm1(float(np.float32(-EPSILON)))))
    a = np.float32(math.exp(-float(dt)))
    powers = [one]
    while powers[-1] * a > np.finfo(np.float32).tiny:
        powers.append(powers[-1] * a)
    return [float(p) for p in powers]


def build(nc, x, x_turned, ctx, patch_lens, w_in, b_in, g_res, g_init, w_r, w_k, w_v, mu_r, mu_k, out):
    B, S, D = x.shape
    DG = ctx.shape[2]
    C = D // P
    T = S // P
    H16, W32 = 16, 32
    LAST = B - 1
    SCAN = 3
    assert D == 512 and S == 512 and DG == 2 * D and B == 16 and H16 * W32 == S
    powers = decay_powers()
    input_gain = math.exp(-EPSILON)

    with ExitStack() as stack:
        def sb(name, shape, dt=F32):
            return stack.enter_context(nc.sbuf_tensor(name, shape, dt))

        def sem(name):
            return stack.enter_context(nc.semaphore(name))

        def sems(names):
            return [sem(name) for name in names.split()]

        bank = [stack.enter_context(nc.psum_tensor(f"bank{i}", [P, 512], F32)) for i in range(8)]

        mask_rows = nc.dram_tensor("mask_rows", [B, S], F32, kind="Internal").ap()
        s_rows = nc.dram_tensor("s_rows", [S, D], F32, kind="Internal").ap()

        wt_hi = [sb(f"w{n}_hi", [P, C, D], F32R) for n in "irkv"]
        wt_lo = [sb(f"w{n}_lo", [P, C, D], F32R) for n in "irkv"]
        WIN, WR, WK, WV = range(4)
        ring = [sb(f"ring{i}", [P, T, D]) for i in range(RING)]
        xt = sb("xt", [P, C, S])
        xt_hi, xt_lo = sb("xt_hi", [P, C, S], F32R), sb("xt_lo", [P, C, S], F32R)
        normed = sb("normed", [P, T, D])
        turned = sb("turned", [P, C, S + 1])
        xk_hi, xk_lo = sb("xk_hi", [P, C, S], F32R), sb("xk_lo", [P, C, S], F32R)
        xr_hi, xr_lo = sb("xr_hi", [P, C, S], F32R), sb("xr_lo", [P, C, S], F32R)
        gate = sb("gate", [P, T, D])
        scratch = sb("scratch", [P, 4, S])
        ctx_rows = sb("ctx_rows", [P, DG])
        u = sb("u", [P, D])
        u_hi, u_lo = sb("u_hi", [P, D], F32R), sb("u_lo", [P, D], F32R)
        scanned, far_scanned = sb("scanned", [P, D]), sb("far_scanned", [P, D])
        bias = sb("bias", [P, D])
        g_ctx = sb("g_ctx", [P, D])
        ident = sb("ident", [P, P])
        average = sb("average", [P, P])
        decay = sb("decay", [P, 2, P])
        decay_hi, decay_lo = sb("decay_hi", [P, 2, P], F32R), sb("decay_lo", [P, 2, P], F32R)
        mus = sb("mus", [P, 4, C])
        g_cols = sb("g_cols", [P, C])
        count_i = sb("count_i", [P, W32], I32)
        half = sb("half", [P, T])
        bn_a, mv_a, v_a, rs_a = (sb(f"{n}_a", [P, T, k]) for n, k in (("bn", 6), ("mv", 2), ("v", 1), ("rs", 1)))
        bn_b, mv_b, v_b, rs_b = (sb(f"{n}_b", [P, T, k]) for n, k in (("bn", 6), ("mv", 2), ("v", 1), ("rs", 1)))
        bn_c, mv_c, v_c, rs_c = (sb(f"{n}_c", [P, k]) for n, k in (("bn", 12), ("mv", 2), ("v", 2), ("rs", 1)))
        far_table = sb("far_table", [1, 2 * B], I32)
        far_f = sb("far_f", [1, 3, B])
        index_i = sb("index_i", [P, 3, T * B], I32)
        patch_of, patch_now = sb("patch_of", [P, B, T], U32), sb("patch_now", [P, T], U32)

        lens = [normed[0:B, 0:2, :].rearrange("p a b -> p (a b)").bitcast(I32),
                normed[0:B, 2:4, :].rearrange("p a b -> p (a b)").bitcast(I32)]
        index_f, index_s = u[0:B, :], far_scanned[0:B, :]
        mask = normed[0:H16, 0, :]
        mask_b, ones_b, sums_b, plug_b = (far_scanned[0:B, :], normed[0:B, 1, :], normed[0:B, 2, :], normed[0:B, 3, :])
        low_hot = scratch[:, 0:2, :].rearrange("p a b -> p (a b)").bitcast(BF16).rearrange("p (n w) -> p n w", w=W32)
        high_hot = scratch[:, 2, :].bitcast(BF16).rearrange("p (n h) -> p n h", h=H16)
        staged = [gate, ring[2], turned[:, :, 1:S + 1], gate]

        lens_loaded, bias_loaded, g_ctx_loaded, mus_loaded, g_loaded = sems("lens_loaded bias_loaded g_ctx_loaded mus_loaded g_loaded")
        w_loaded = [sem(f"w_loaded{i}") for i in range(4)]
        x_loaded = [sem(f"x_loaded{i}") for i in range(RING)]
        xt_loaded, ctx_loaded = sems("xt_loaded ctx_loaded")
        half_ready, ident_ready, average_ready, counts_ready, decay_ready, decay_hi_ready, decay_lo_ready = sems(
            "half_ready ident_ready average_ready counts_ready decay_ready decay_hi_ready decay_lo_ready")
        zero_ready, zeros_ready, s_zeroed, g_ready, mus_ready = sems("zero_ready zeros_ready s_zeroed g_ready mus_ready")
        pad_ready, plug_step, index_turned, hots_ready, mask_counted, mask_copied, mask_stored, mask_loaded = sems(
            "pad_ready plug_step index_turned hots_ready mask_counted mask_copied mask_stored mask_loaded")
        plug_turned, patches_ready, table_ready = sems("plug_turned patches_ready table_ready")
        g_applied, w_averaged, w_centred, w_hi_ready, w_lo_ready = sems("g_applied w_averaged w_centred w_hi_ready w_lo_ready")
        bn_a_done, mv_a_done, v_a_done, rs_a_done, xb_ready = sems("bn_a_done mv_a_done v_a_done rs_a_done xb_ready")
        xt_hi_ready, xt_lo_ready, proj_done, x2_ready = sems("xt_hi_ready xt_lo_ready proj_done x2_ready")
        bn_c_done, mv_c_done, ms_c_done, v_c_done, rs_c_done = sems("bn_c_done mv_c_done ms_c_done v_c_done rs_c_done")
        u_ready, u_hi_ready, u_lo_ready, s_done, s_copied, s_stored, patch_picked, dep_added = sems(
            "u_ready u_hi_ready u_lo_ready s_done s_copied s_stored patch_picked dep_added")
        far_loaded, far_bn, far_mv, far_ms, far_v, far_rs, far_u, far_u_hi, far_u_lo = sems(
            "far_loaded far_bn far_mv far_ms far_v far_rs far_u far_u_hi far_u_lo")
        far_carried, far_s, far_copied, far_stored, far_over = sems("far_carried far_s far_copied far_stored far_over")
        bn_b_done, mv_b_done, v_b_done, rs_b_done, yn_ready, yn_turned, yt_ready = sems(
            "bn_b_done mv_b_done v_b_done rs_b_done yn_ready yn_turned yt_ready")
        carried, mixed, mix_hi_ready, mix_lo_ready = sems("carried mixed mix_hi_ready mix_lo_ready")
        r_done, gate_ready, k_done, relu_ready, square_ready, ka_hi_ready, ka_lo_ready = sems(
            "r_done gate_ready k_done relu_ready square_ready ka_hi_ready ka_lo_ready")
        v_done, gated, out_ready = sems("v_done gated out_ready")
        stored = [sem(f"stored{t}") for t in range(T)]
        dve_passed, pool_passed = sems("dve_passed pool_passed")

        def f32(ap):
            return ap.bitcast(F32)

        def tile(t):
            return slice(t * P, (t + 1) * P)

        def is_first(b, n=0):
            return b.fixed and b.number() == n

        def is_last(b):
            return b.fixed and b.number() == LAST

        def ka(b):
            return (xt_hi, xt_lo) if is_last(b) else (xr_hi, xr_lo)

        def scan_bank(b):
            return bank[7 if is_first(b) else SCAN]

        def mix_row(b, i):
            return (1 - i // C if is_last(b) else i // C), i % C

        x_rows = x.rearrange("b (t p) d -> b p t d", p=P)
        xt_rows = x_turned.rearrange("b (c p) s -> b p c s", p=P)
        out_rows = out.rearrange("b (t p) d -> b p t d", p=P)

        def far_count(eng, b):
            n = b.number()
            return (eng.value_load(far_table[0:1, bass.ds(n, 1)], min_val=0, max_val=1),
                    eng.value_load(far_table[0:1, bass.ds(n + B, 1)], min_val=0, max_val=B - 1))

        SHIFTS = [1 << k for k in range(S.bit_length() - 1)]
        PAD = S // 2
        INDEX_STEP = len(SHIFTS) + 4
        PLUG_STEP = INDEX_STEP + 3 + 2

        block = stack.enter_context(nc.Block())

        @block.sync
        def _(sp):
            def load_w(w, rows):
                sp.dma_start(staged[w][:, :, :], rows.rearrange("(c p) d -> p c d", p=P)).then_inc(w_loaded[w], 16)

            def load_x(b):
                sp.dma_start(ring[b.slot][:, :, :], x_rows[b.number()]).then_inc(x_loaded[b.slot], 16)

            def load_xt(b):
                sp.dma_start(xt[:, :, :], xt_rows[b.number()]).then_inc(xt_loaded, 16)

            def load_ctx(b):
                sp.dma_start(ctx_rows[:, :], ctx[b.number(), 0:P, :]).then_inc(ctx_loaded, 16)

            sp.dma_start(lens[0][:, PAD:PAD + S], patch_lens).then_inc(lens_loaded, 16)
            load_w(WIN, w_in)
            load_xt(Batch(0, 0))
            load_x(Batch(0, 0))
            load_ctx(Batch(0, 0))
            load_w(WR, w_r)
            load_w(WK, w_k)
            sp.wait_ge(w_lo_ready, C)
            load_w(WV, w_v)

            def iteration(b):
                new = b.plus(2)
                if new.exists(B):
                    if not is_first(new):
                        reached(sp, xt_lo_ready, new.plus(-1), 2, 2)
                        load_xt(new)
                        reached(sp, out_ready, b.plus(-1), T, T)
                        if is_first(new, 2):
                            sp.wait_ge(w_lo_ready, 2 * C)
                        load_x(new)
                        reached(sp, far_over, new.plus(-1), 1, 1)
                        load_ctx(new)
                if b.exists(B):
                    for t in range(T):
                        reached(sp, out_ready, b, T, t + 1)
                        sp.dma_start(out_rows[b.number(), :, t, :], gate[:, t, :]).then_inc(stored[t], 16)

            batches(sp, iteration, B)
            for t in range(T):
                sp.wait_ge(stored[t], 16 * B)

        @block.gpsimd
        def _(pool):
            nc.gpsimd.memset(scanned[:, :], 0.0).then_inc(zeros_ready, 1)
            for n in range(2):
                nc.gpsimd.memset(lens[n][:, 0:PAD], 0).then_inc(pad_ready, 1)
            nc.gpsimd.memset(half[:, :], -0.5).then_inc(half_ready, 1)
            nc.gpsimd.memset(average[:, :], 1.0 / D).then_inc(average_ready, 1)
            nc.gpsimd.memset(ident[:, :], 0.0).then_inc(ident_ready, 1)
            pool.wait_ge(ident_ready, 1)
            nc.gpsimd.affine_select(out=ident[:, :], in_=ident[:, :], compare_op=ALU.not_equal, fill=1.0, base=0,
                                    pattern=[[-1, P]], channel_multiplier=1).then_inc(ident_ready, 1)
            nc.gpsimd.iota(count_i[:, :], pattern=[[1, W32]], base=0, channel_multiplier=0).then_inc(counts_ready, 1)

            def make_decay():
                nc.gpsimd.memset(decay[:, :, :], 0.0).then_inc(decay_ready, 1)
                steps = 1
                for which, base in ((0, 0), (1, P)):
                    for k, value in enumerate(powers):
                        if which == 1 and k == 0:
                            continue
                        pool.wait_ge(decay_ready, steps)
                        nc.gpsimd.affine_select(out=decay[:, which, :], in_=decay[:, which, :],
                                                compare_op=ALU.not_equal, fill=value, base=base - k,
                                                pattern=[[1, P]], channel_multiplier=-1).then_inc(decay_ready, 1)
                        steps += 1

            def far(b):
                n = far_count(pool, b)
                with pool.If(n[0] > 0):
                    for c in range(1, T):
                        done = n[1] * (T - 1) + c
                        if c == 1:
                            reached(pool, u_ready, b, 1, 1)
                        else:
                            pool.wait_ge(far_u, done - 1)
                        hold(pool, pool_passed)
                        pool.dma_start(ctx_rows[:, :], ctx[b.number(), c * P:(c + 1) * P, :]).then_inc(far_loaded, 16)
                        pool.wait_ge(far_v, done)
                        nc.gpsimd.tensor_tensor(rs_c[:, :], v_c[:, 1:2], half[:, 0:1], ALU.pow).then_inc(far_rs, 1)
                        pool.wait_ge(far_copied, done)
                        hold(pool, pool_passed)
                        pool.dma_start(s_rows[c * P:(c + 1) * P, :],
                                       far_scanned[:, :]).then_inc(far_stored, 16)
                        pool.wait_ge(far_stored, done * 16)
                        hold(pool, pool_passed)

            def add_patches(b):
                if not is_first(b):
                    reached(pool, dep_added, b.plus(-1), T * 16, T * 16)
                nc.gpsimd.tensor_copy(patch_now[:, :], patch_of[:, bass.ds(b.number(), 1), :].rearrange("p a t -> p (a t)")
                                      ).then_inc(patch_picked, 1)
                reached(pool, xb_ready, b, 1, 1)
                reached(pool, s_stored, b, 16, 16)
                reached(pool, patch_picked, b, 1, 1)
                hold(pool, pool_passed)
                for t in range(T):
                    pool.indirect_dma_start(ring[b.slot][:, t, :], None, s_rows[:, :],
                                            bass.IndirectOffsetOnAxis(ap=patch_now[:, t:t + 1], axis=0),
                                            compute_op=ALU.add).then_inc(dep_added, 16)

            def add_out(b, t):
                reached(pool, gated, b, T, t + 1)
                nc.gpsimd.tensor_tensor(gate[:, t, :], gate[:, t, :], ring[b.slot][:, t, :], ALU.add).then_inc(out_ready, 1)

            def iteration(b):
                nxt, new = b.plus(1), b.plus(2)
                if nxt.exists(B):
                    reached(pool, v_b_done, nxt, 1, 1)
                    reached(pool, yn_ready, b, T, T)
                    nc.gpsimd.tensor_tensor(rs_b[:, :, 0], v_b[:, :, 0], half[:, :], ALU.pow).then_inc(rs_b_done, 1)
                if new.exists(B):
                    if is_first(new):
                        pool.wait_ge(half_ready, 1)
                    reached(pool, v_a_done, new, 1, 1)
                    reached(pool, x2_ready, nxt, T, T)
                    nc.gpsimd.tensor_tensor(rs_a[:, :, 0], v_a[:, :, 0], half[:, :], ALU.pow).then_inc(rs_a_done, 1)
                    reached(pool, v_c_done, new, 1, 1)
                    reached(pool, u_ready, nxt, 1, 1)
                    nc.gpsimd.tensor_tensor(rs_c[:, :], v_c[:, 1:2], half[:, 0:1], ALU.pow).then_inc(rs_c_done, 1)
                    if is_first(new):
                        make_decay()
                        pool.wait_ge(bias_loaded, 16)
                    reached(pool, bn_a_done, new, T, T)
                    nc.gpsimd.tensor_tensor(ring[new.slot][:, :, :], ring[new.slot][:, :, :],
                                            bias[:, :].unsqueeze(1).to_broadcast([P, T, D]), ALU.add).then_inc(xb_ready, 1)
                if b.exists(B):
                    add_out(b, 0)
                    add_out(b, 1)
                if new.exists(B):
                    if is_first(new):
                        pool.wait_ge(table_ready, 2)
                        pool.wait_ge(patches_ready, 1)
                        pool.wait_ge(s_zeroed, 16 * (T - 1))
                    far(new)
                    add_patches(new)
                if b.exists(B):
                    add_out(b, 2)
                    add_out(b, 3)

            batches(pool, iteration, B)

        @block.tensor
        def _(pe):
            def product(where, lhs_hi, lhs_lo, rhs_hi, rhs_lo, start, stop):
                nc.tensor.matmul(where, lhs_hi, rhs_hi, start=start, stop=False)
                nc.tensor.matmul(where, lhs_hi, rhs_lo, start=False, stop=False)
                return nc.tensor.matmul(where, lhs_lo, rhs_hi, start=False, stop=stop)

            def project(b):
                for t in range(T):
                    if t == 0:
                        reached(pe, xt_lo_ready, b, 2, 2)
                        reached(pe, yt_ready, b.plus(-1), T, T)
                    for c in range(C):
                        last = product(bank[t][:, :], xt_hi[:, c, tile(t)], xt_lo[:, c, tile(t)],
                                       wt_hi[WIN][:, c, :], wt_lo[WIN][:, c, :], c == 0, c == C - 1)
                    last.then_inc(proj_done, 1)

            def scan(b):
                reached(pe, u_lo_ready, b, 1, 1)
                if is_first(b):
                    pe.wait_ge(decay_lo_ready, 1)
                    pe.wait_ge(w_centred, C)
                if is_first(b, 1):
                    reached(pe, x2_ready, b.plus(-1), T, T)
                    reached(pe, s_copied, b.plus(-1), 1, 1)
                product(scan_bank(b)[:, :], decay_hi[:, 0, :], decay_lo[:, 0, :], u_hi[:, :], u_lo[:, :],
                        True, True).then_inc(s_done, 1)
                if is_first(b):
                    pe.wait_ge(table_ready, 2)
                far(b)

            def far(b):
                n = far_count(pe, b)
                with pe.If(n[0] > 0):
                    for c in range(1, T):
                        done = n[1] * (T - 1) + c
                        if c > 1:
                            pe.wait_ge(far_copied, done - 1)
                        else:
                            reached(pe, s_copied, b, 1, 1)
                        product(scan_bank(b)[:, :], decay_hi[:, 1, :], decay_lo[:, 1, :], u_hi[:, :], u_lo[:, :],
                                True, False).then_inc(far_carried, 1)
                        pe.wait_ge(far_u_lo, done)
                        product(scan_bank(b)[:, :], decay_hi[:, 0, :], decay_lo[:, 0, :], u_hi[:, :], u_lo[:, :],
                                False, True).then_inc(far_s, 1)

            def gate_product(b):
                for t in range(T):
                    reached(pe, gated, b.plus(-1), T, t + 1)
                    reached(pe, mix_lo_ready, b, 2 * C, 2 * C if is_last(b) else C)
                    if is_first(b):
                        pe.wait_ge(w_lo_ready, 2 * C)
                    for c in range(C):
                        last = product(bank[4 + t][:, :], xr_hi[:, c, tile(t)], xr_lo[:, c, tile(t)],
                                       wt_hi[WR][:, c, :], wt_lo[WR][:, c, :], c == 0, c == C - 1)
                    last.then_inc(r_done, 1)

            def key_product(b):
                for m in range(C):
                    reached(pe, mix_lo_ready, b, 2 * C, C if is_last(b) else 2 * C)
                    if is_first(b):
                        pe.wait_ge(w_lo_ready, 3 * C)
                    if is_last(b):
                        reached(pe, yt_ready, b, T, T)
                    else:
                        reached(pe, x2_ready, b.plus(1), T, m + 1)
                    for c in range(C):
                        last = product(bank[m][:, :], wt_hi[WK][:, c, tile(m)], wt_lo[WK][:, c, tile(m)],
                                       xk_hi[:, c, :], xk_lo[:, c, :], c == 0, c == C - 1)
                    last.then_inc(k_done, 1)

            def value_product(b, t, first, last):
                ka_hi, ka_lo = ka(b)
                if first == 0:
                    reached(pe, gate_ready, b, T, t + 1)
                    if is_first(b) and t == 0:
                        pe.wait_ge(w_lo_ready, 4 * C)
                for m in range(first, last):
                    if t == 0:
                        reached(pe, ka_lo_ready, b, C, m + 1)
                    done = product(bank[4 + t][:, :], ka_hi[:, m, tile(t)], ka_lo[:, m, tile(t)],
                                   wt_hi[WV][:, m, :], wt_lo[WV][:, m, :], m == 0, m == C - 1)
                if last == C:
                    done.then_inc(v_done, 1)

            def turn(b):
                for t in range(T):
                    reached(pe, yn_ready, b, T, t + 1)
                    if b.plus(-1).exists(B):
                        reached(pe, relu_ready, b.plus(-1), C, t + 1)
                    if t == SCAN and b.plus(1).exists(B):
                        reached(pe, s_copied, b.plus(1), 1, 1)
                        reached(pe, far_over, b.plus(1), 1, 1)
                    for c in range(C):
                        last = nc.tensor.transpose(bank[t][:, tile(c)], normed[:, t, c * P:(c + 1) * P], ident[:, :])
                    last.then_inc(yn_turned, 1)

            def iteration(b):
                nxt, new = b.plus(1), b.plus(2)
                if nxt.exists(B) and not is_first(nxt):
                    project(nxt)
                if b.exists(B) and not is_last(b):
                    gate_product(b)
                    key_product(b)
                    if is_last(nxt):
                        turn(nxt)
                    value_product(b, 0, 0, C - 1)
                    value_product(b, 1, 0, C - 1)
                    value_product(b, 0, C - 1, C)
                    value_product(b, 1, C - 1, C)
                if is_last(b):
                    key_product(b)
                    gate_product(b)
                    for t in range(T):
                        value_product(b, t, 0, C)
                if new.exists(B):
                    scan(new)
                if b.exists(B) and not is_last(b):
                    for t in range(2, T):
                        value_product(b, t, 0, C)
                if nxt.exists(B) and not is_last(nxt):
                    turn(nxt)

            pe.wait_ge(g_applied, C)
            pe.wait_ge(average_ready, 1)
            for c in range(C):
                last = nc.tensor.matmul(bank[7][:, :], average[:, :], staged[WIN][:, c, :], start=c == 0, stop=c == C - 1)
            last.then_inc(w_averaged, 1)

            pe.wait_ge(ident_ready, 2)
            pe.wait_ge(plug_step, INDEX_STEP)
            for j in range(T):
                last = nc.tensor.transpose(bank[5][:, j * B:(j + 1) * B], index_f[:, tile(j)], ident[0:B, 0:B])
            last.then_inc(index_turned, 1)
            pe.wait_ge(hots_ready, 2)
            for n in range(B):
                for j in range(T):
                    last = nc.tensor.matmul(bank[4][0:H16, n * W32:(n + 1) * W32], high_hot[:, j * B + n, :],
                                            low_hot[:, j * B + n, :], start=j == 0, stop=j == T - 1)
            last.then_inc(mask_counted, 1)
            project(Batch(0, 0))
            pe.wait_ge(plug_step, PLUG_STEP)
            for j in range(T):
                nc.tensor.transpose(bank[6][:, j * B:(j + 1) * B], plug_b[:, tile(j)], ident[0:B, 0:B])
            nc.tensor.matmul(bank[5][0:1, 0:B], plug_b[:, S - 1:S], ident[0:B, 0:B], start=True,
                             stop=True).then_inc(plug_turned, 1)

            batches(pe, iteration, B)

        @block.scalar
        def _(act):
            def copy(to, of):
                return nc.scalar.activation(to, of, ACT.Copy)

            def weight_hi(w):
                for c in range(C):
                    if w == WIN:
                        act.wait_ge(w_centred, c + 1)
                    else:
                        act.wait_ge(w_loaded[w], 16)
                    copy(wt_hi[w][:, c, :], staged[w][:, c, :]).then_inc(w_hi_ready, 1)

            def x_hi(b):
                reached(act, xt_loaded, b, 16, 16)
                reached(act, proj_done, b.plus(-1), T, T)
                for n in range(2):
                    copy(xt_hi[:, 2 * n:2 * n + 2, :], xt[:, 2 * n:2 * n + 2, :]).then_inc(xt_hi_ready, 1)

            def mix_hi(b, first, last):
                for i in range(first, last):
                    which, c = mix_row(b, i)
                    reached(act, mixed, b, 2 * C, i + 1)
                    if i == 0:
                        reached(act, k_done, b.plus(-1), C, C)
                    if which == 0 and c == 0:
                        reached(act, v_done, b.plus(-1), T, T)
                    copy((xr_hi, xk_hi)[which][:, c, :], scratch[:, 2 + i % 2, :]).then_inc(mix_hi_ready, 1)

            def gates(b):
                for t in range(T):
                    reached(act, r_done, b, T, t + 1)
                    reached(act, stored[t], b, 16, 0)
                    if is_first(b):
                        act.wait_ge(w_lo_ready, 4 * C)
                    nc.scalar.activation(gate[:, t, :], bank[4 + t][:, :], ACT.Sigmoid).then_inc(gate_ready, 1)

            def squares(b):
                for m in range(C):
                    reached(act, k_done, b, C, m + 1)
                    if m == 0:
                        reached(act, mix_lo_ready, b, 2 * C, 2 * C)
                    if m >= 2:
                        reached(act, ka_lo_ready, b, C, m - 1)
                    nc.scalar.activation(scratch[:, m % 2, :], bank[m][:, :], ACT.Relu).then_inc(relu_ready, 1)
                    reached(act, relu_ready, b, C, m + 1)
                    nc.scalar.activation(scratch[:, 2 + m % 2, :], scratch[:, m % 2, :], ACT.Square).then_inc(square_ready, 1)
                    reached(act, square_ready, b, C, m + 1)
                    copy(ka(b)[0][:, m, :], scratch[:, 2 + m % 2, :]).then_inc(ka_hi_ready, 1)

            def turned_out(b):
                for t in range(T):
                    reached(act, yn_turned, b, T, t + 1)
                    if t == 0:
                        reached(act, mix_lo_ready, b.plus(-1), 2 * C, 2 * C)
                        if is_first(b):
                            act.wait_ge(w_lo_ready, 3 * C)
                    copy(turned[:, :, 1 + t * P:1 + (t + 1) * P],
                         bank[t][:, :].rearrange("p (c n) -> p c n", c=C)).then_inc(yt_ready, 1)

            def iteration(b):
                nxt, new = b.plus(1), b.plus(2)
                if b.exists(B):
                    if is_last(b):
                        mix_hi(b, C, 2 * C)
                        squares(b)
                        gates(b)
                    else:
                        mix_hi(b, 0, 2 * C)
                        gates(b)
                if new.exists(B):
                    if is_first(new):
                        for w in (WR, WK):
                            weight_hi(w)
                        act.wait_ge(decay_ready, 2 * len(powers))
                        copy(decay_hi[:, :, :], decay[:, :, :]).then_inc(decay_hi_ready, 1)
                    else:
                        x_hi(new)
                if b.exists(B) and not is_last(b):
                    squares(b)
                if is_last(nxt):
                    turned_out(nxt)
                    mix_hi(nxt, 0, C)
                if new.exists(B):
                    reached(act, u_ready, new, 1, 1)
                    reached(act, far_over, new.plus(-1), 1, 1)
                    reached(act, s_done, new.plus(-1), 1, 1)
                    copy(u_hi[:, :], u[:, :]).then_inc(u_hi_ready, 1)
                    reached(act, s_done, new, 1, 1)
                    if is_first(new):
                        act.wait_ge(s_zeroed, 16 * (T - 1))
                    reached(act, s_stored, new, 16, 0)
                    copy(scanned[:, :], scan_bank(new)[:, :]).then_inc(s_copied, 1)
                    reached(act, s_copied, new, 1, 1)
                    reached(act, dep_added, new.plus(-1), T * 16, T * 16)
                    act.dma_start(s_rows[0:P, :], scanned[:, :]).then_inc(s_stored, 16)
                    if is_first(new):
                        weight_hi(WV)
                if nxt.exists(B) and not is_last(nxt):
                    turned_out(nxt)

            act.dma_start(g_cols[:, :], g_res.rearrange("(c p) -> p c", p=P),
                          allow_slow_non_contiguous=True).then_inc(g_loaded, 16)
            act.dma_start(bias[:, :], b_in.partition_broadcast(P)).then_inc(bias_loaded, 16)
            act.dma_start(g_ctx[:, :], g_init[0:D].partition_broadcast(P)).then_inc(g_ctx_loaded, 16)
            for n, mu in enumerate((mu_r, mu_k)):
                act.dma_start(mus[:, n, :], mu.rearrange("(c p) -> p c", p=P),
                              allow_slow_non_contiguous=True).then_inc(mus_loaded, 16)
            act.wait_ge(zeros_ready, 1)
            for n in range(1, T):
                act.dma_start(s_rows[tile(n), :], scanned[:, :]).then_inc(s_zeroed, 16)
            x_hi(Batch(0, 0))
            weight_hi(WIN)
            act.wait_ge(mask_copied, 1)
            act.dma_start(mask_rows.rearrange("b (h w) -> h b w", w=W32),
                          mask.rearrange("h (b w) -> h b w", w=W32)).then_inc(mask_stored, 16)
            act.wait_ge(mask_stored, 16)
            act.dma_start(mask_b, mask_rows).then_inc(mask_loaded, 16)
            batches(act, iteration, B)

        @block.vector
        def _(dve):
            steps = [0]

            def step(instruction):
                instruction.then_inc(plug_step, 1)
                steps[0] += 1
                dve.wait_ge(plug_step, steps[0])

            def low(to, whole, high):
                return nc.vector.tensor_tensor(to, whole, high, ALU.subtract)

            def weight_lo(w):
                for c in range(C):
                    dve.wait_ge(w_hi_ready, w * C + c + 1)
                    low(wt_lo[w][:, c, :], staged[w][:, c, :], f32(wt_hi[w][:, c, :])).then_inc(w_lo_ready, 1)

            def x_lo(b):
                for n in range(2):
                    reached(dve, xt_hi_ready, b, 2, n + 1)
                    low(xt_lo[:, 2 * n:2 * n + 2, :], xt[:, 2 * n:2 * n + 2, :],
                        f32(xt_hi[:, 2 * n:2 * n + 2, :])).then_inc(xt_lo_ready, 1)

            def stats_a(b):
                dve.wait_ge(x_loaded[b.slot], (b.round() + 1) * 16)
                for t in range(T):
                    nc.vector.bn_stats(bn_a[:, t, :], ring[b.slot][:, t, :]).then_inc(bn_a_done, 1)
                reached(dve, bn_a_done, b, T, T)
                hold(dve, dve_passed)
                for t in range(T):
                    nc.vector.bn_aggr(mv_a[:, t, :], bn_a[:, t, :]).then_inc(mv_a_done, 1)
                reached(dve, mv_a_done, b, T, T)
                nc.vector.tensor_scalar(v_a[:, :, 0], mv_a[:, :, 1], 1.0 + RMS_EPS, RMS_EPS * LN_EPS,
                                        ALU.mult, ALU.add).then_inc(v_a_done, 1)

            def stats_c(b):
                reached(dve, ctx_loaded, b, 16, 16)
                for h in range(2):
                    nc.vector.bn_stats(bn_c[:, 6 * h:6 * h + 6], ctx_rows[:, h * D:(h + 1) * D]).then_inc(bn_c_done, 1)
                reached(dve, bn_c_done, b, 2, 2)
                hold(dve, dve_passed)
                nc.vector.bn_aggr(mv_c[:, :], bn_c[:, :]).then_inc(mv_c_done, 1)
                reached(dve, mv_c_done, b, 1, 1)
                nc.vector.scalar_tensor_tensor(v_c[:, 0:1], mv_c[:, 0:1], mv_c[:, 0:1], mv_c[:, 1:2],
                                               ALU.mult, ALU.add).then_inc(ms_c_done, 1)
                reached(dve, ms_c_done, b, 1, 1)
                nc.vector.tensor_scalar(v_c[:, 1:2], v_c[:, 0:1], RMS_EPS, None, ALU.add).then_inc(v_c_done, 1)

            def scan_input(b):
                reached(dve, rs_c_done, b, 1, 1)
                reached(dve, u_lo_ready, b.plus(-1), 1, 1)
                nc.vector.scalar_tensor_tensor(u[:, :], ctx_rows[:, 0:D], rs_c[:, :], g_ctx[:, :],
                                               ALU.mult, ALU.mult).then_inc(u_ready, 1)

            def far(b):
                n = far_count(dve, b)
                with dve.If(n[0] > 0):
                    for c in range(1, T):
                        done = n[1] * (T - 1) + c
                        dve.wait_ge(far_loaded, done * 16)
                        for h in range(2):
                            nc.vector.bn_stats(bn_c[:, 6 * h:6 * h + 6], ctx_rows[:, h * D:(h + 1) * D]).then_inc(far_bn, 1)
                        dve.wait_ge(far_bn, done * 2)
                        hold(dve, dve_passed)
                        nc.vector.bn_aggr(mv_c[:, :], bn_c[:, :]).then_inc(far_mv, 1)
                        dve.wait_ge(far_mv, done)
                        nc.vector.scalar_tensor_tensor(v_c[:, 0:1], mv_c[:, 0:1], mv_c[:, 0:1], mv_c[:, 1:2],
                                                       ALU.mult, ALU.add).then_inc(far_ms, 1)
                        dve.wait_ge(far_ms, done)
                        nc.vector.tensor_scalar(v_c[:, 1:2], v_c[:, 0:1], RMS_EPS, None, ALU.add).then_inc(far_v, 1)
                        dve.wait_ge(far_rs, done)
                        nc.vector.scalar_tensor_tensor(u[:, :], ctx_rows[:, 0:D], rs_c[:, :], g_ctx[:, :],
                                                       ALU.mult, ALU.mult).then_inc(far_u, 1)
                        dve.wait_ge(far_u, done)
                        dve.wait_ge(far_carried, done)
                        nc.vector.tensor_copy(u_hi[:, :], u[:, :]).then_inc(far_u_hi, 1)
                        dve.wait_ge(far_u_hi, done)
                        low(u_lo[:, :], u[:, :], f32(u_hi[:, :])).then_inc(far_u_lo, 1)
                        dve.wait_ge(far_s, done)
                        if c > 1:
                            dve.wait_ge(far_stored, (done - 1) * 16)
                        nc.vector.tensor_copy(far_scanned[:, :], scan_bank(b)[:, :]).then_inc(far_copied, 1)
                    dve.wait_ge(far_copied, n[1] * (T - 1) + T - 1)
                    hold(dve, dve_passed)

            def carry(b, i):
                which, c = mix_row(b, i)
                nc.vector.tensor_scalar(scratch[:, i % 2, :], turned[:, c, 0:S], mus[:, 2 + which, c:c + 1], None,
                                        ALU.mult).then_inc(carried, 1)

            def mix(b, i):
                which, c = mix_row(b, i)
                reached(dve, carried, b, 2 * C, i + 1)
                nc.vector.scalar_tensor_tensor(scratch[:, 2 + i % 2, :], turned[:, c, 1:S + 1],
                                               mus[:, which, c:c + 1], scratch[:, i % 2, :],
                                               ALU.mult, ALU.add).then_inc(mixed, 1)

            def mix_low(b, i):
                which, c = mix_row(b, i)
                reached(dve, mix_hi_ready, b, 2 * C, i + 1)
                hi, lo = ((xr_hi, xr_lo), (xk_hi, xk_lo))[which]
                low(lo[:, c, :], scratch[:, 2 + i % 2, :], f32(hi[:, c, :])).then_inc(mix_lo_ready, 1)

            def mixing(b, first, last):
                for i in range(first, last):
                    if i == 0:
                        reached(dve, yt_ready, b, T, T)
                        carry(b, 0)
                    else:
                        reached(dve, mixed, b, 2 * C, i)
                    if i + 1 < 2 * C:
                        carry(b, i + 1)
                    if i >= 2:
                        reached(dve, mix_lo_ready, b, 2 * C, i - 1)
                    mix(b, i)
                    if i >= 1:
                        mix_low(b, i - 1)
                if last == 2 * C:
                    mix_low(b, last - 1)

            def add_x(b, t):
                reached(dve, proj_done, b, T, t + 1)
                if t == 0:
                    reached(dve, dep_added, b, T * 16, T * 16)
                    reached(dve, rs_a_done, b, 1, 1)
                nc.vector.scalar_tensor_tensor(ring[b.slot][:, t, :], bank[t][:, :], rs_a[:, t, :], ring[b.slot][:, t, :],
                                               ALU.mult, ALU.add).then_inc(x2_ready, 1)

            def stats_b(b):
                for t in range(T):
                    reached(dve, x2_ready, b, T, t + 1)
                    nc.vector.bn_stats(bn_b[:, t, :], ring[b.slot][:, t, :]).then_inc(bn_b_done, 1)
                reached(dve, bn_b_done, b, T, T)
                hold(dve, dve_passed)
                for t in range(T):
                    nc.vector.bn_aggr(mv_b[:, t, :], bn_b[:, t, :]).then_inc(mv_b_done, 1)
                reached(dve, mv_b_done, b, T, T)
                nc.vector.tensor_scalar(v_b[:, :, 0], mv_b[:, :, 1], LN_EPS, None, ALU.add).then_inc(v_b_done, 1)

            def norm_b(b):
                reached(dve, rs_b_done, b, 1, 1)
                reached(dve, yn_turned, b.plus(-1), T, T)
                for t in range(T):
                    nc.vector.tensor_scalar(normed[:, t, :], ring[b.slot][:, t, :], mv_b[:, t, 0:1], rs_b[:, t, :],
                                            ALU.subtract, ALU.mult).then_inc(yn_ready, 1)

            def gating(b, t):
                reached(dve, v_done, b, T, t + 1)
                reached(dve, gate_ready, b, T, t + 1)
                nc.vector.tensor_tensor(gate[:, t, :], bank[4 + t][:, :], gate[:, t, :], ALU.mult).then_inc(gated, 1)

            def iteration(b):
                nxt, new = b.plus(1), b.plus(2)
                if b.exists(B):
                    mixing(b, C if is_last(b) else 0, 2 * C if is_last(b) else C + 1)
                if nxt.exists(B):
                    add_x(nxt, 0)
                    add_x(nxt, 1)
                if b.exists(B) and not is_last(b):
                    mixing(b, C + 1, 2 * C - 1)
                if nxt.exists(B):
                    add_x(nxt, 2)
                if b.exists(B) and not is_last(b):
                    mixing(b, 2 * C - 1, 2 * C)
                if nxt.exists(B):
                    add_x(nxt, 3)
                    stats_b(nxt)
                if new.exists(B) and not is_first(new):
                    stats_a(new)
                    stats_c(new)
                if nxt.exists(B):
                    norm_b(nxt)
                if new.exists(B) and not is_first(new):
                    x_lo(new)
                    scan_input(new)
                if b.exists(B):
                    for m in range(C):
                        ka_hi, ka_lo = ka(b)
                        reached(dve, ka_hi_ready, b, C, m + 1)
                        low(ka_lo[:, m, :], scratch[:, 2 + m % 2, :], f32(ka_hi[:, m, :])).then_inc(ka_lo_ready, 1)
                if is_last(nxt):
                    mixing(nxt, 0, C)
                if new.exists(B):
                    reached(dve, u_hi_ready, new, 1, 1)
                    low(u_lo[:, :], u[:, :], f32(u_hi[:, :])).then_inc(u_lo_ready, 1)
                if b.exists(B):
                    gating(b, 0)
                    gating(b, 1)
                if new.exists(B):
                    reached(dve, u_lo_ready, new, 1, 1)
                    if is_first(new):
                        dve.wait_ge(table_ready, 2)
                    far(new)
                    dve.sem_inc(far_over, 1)
                if b.exists(B):
                    gating(b, 2)
                    gating(b, 3)
                if is_first(new):
                    weight_lo(WV)

            dve.wait_ge(lens_loaded, 16)
            dve.wait_ge(pad_ready, 2)
            here, there = lens
            for shift in SHIFTS:
                step(nc.vector.tensor_tensor(there[:, PAD:PAD + S], here[:, PAD:PAD + S],
                                             here[:, PAD - shift:PAD + S - shift], ALU.add))
                here, there = there, here
            step(nc.vector.tensor_scalar(index_f, here[:, PAD:PAD + S], -1.0, None, ALU.add))
            step(nc.vector.tensor_scalar(index_s, index_f, 0.0, float(S), ALU.is_lt, ALU.mult))
            step(nc.vector.tensor_tensor(index_s, index_f, index_s, ALU.add))
            step(nc.vector.tensor_scalar(index_f, index_s, -1.0, float(2 * S - 1), ALU.max, ALU.min))
            assert steps[0] == INDEX_STEP

            dve.wait_ge(g_loaded, 16)
            dve.wait_ge(w_loaded[WIN], 16)
            for c in range(C):
                nc.vector.tensor_scalar(staged[WIN][:, c, :], staged[WIN][:, c, :], g_cols[:, c:c + 1], None,
                                        ALU.mult).then_inc(g_applied, 1)

            dve.wait_ge(counts_ready, 1)
            dve.wait_ge(index_turned, 1)
            step(nc.vector.tensor_copy(index_i[:, 0, :], bank[5][:, 0:T * B]))
            step(nc.vector.tensor_scalar(index_i[:, 1, :], index_i[:, 0, :], 5, None, ALU.arith_shift_right))
            step(nc.vector.tensor_scalar(index_i[:, 2, :], index_i[:, 0, :], W32 - 1, None, ALU.bitwise_and))
            nc.vector.tensor_tensor(high_hot, index_i[:, 1, :].unsqueeze(2).to_broadcast([P, T * B, H16]),
                                    count_i[:, 0:H16].unsqueeze(1).to_broadcast([P, T * B, H16]),
                                    ALU.is_equal).then_inc(hots_ready, 1)
            nc.vector.tensor_tensor(low_hot, index_i[:, 2, :].unsqueeze(2).to_broadcast([P, T * B, W32]),
                                    count_i[:, :].unsqueeze(1).to_broadcast([P, T * B, W32]),
                                    ALU.is_equal).then_inc(hots_ready, 1)

            dve.wait_ge(w_averaged, 1)
            for c in range(C):
                nc.vector.tensor_tensor(staged[WIN][:, c, :], staged[WIN][:, c, :], bank[7][:, :],
                                        ALU.subtract).then_inc(w_centred, 1)
            dve.wait_ge(mask_counted, 1)
            nc.vector.tensor_scalar(mask, bank[4][0:H16, :], 1.0, None, ALU.min).then_inc(mask_copied, 1)
            weight_lo(WIN)
            x_lo(Batch(0, 0))
            nc.vector.memset(ones_b, 1.0).then_inc(zero_ready, 1)
            stats_a(Batch(0, 0))
            dve.wait_ge(g_ctx_loaded, 16)
            nc.vector.tensor_scalar(g_ctx[:, :], g_ctx[:, :], input_gain, None, ALU.mult).then_inc(g_ready, 1)
            stats_c(Batch(0, 0))
            dve.wait_ge(mask_loaded, 16)
            dve.wait_ge(zero_ready, 1)
            step(nc.vector.tensor_tensor_scan(sums_b, ones_b, mask_b, 0.0, ALU.mult, ALU.add))
            step(nc.vector.tensor_scalar(plug_b, sums_b, -1.0, 0.0, ALU.add, ALU.max))
            assert steps[0] == PLUG_STEP
            dve.wait_ge(g_ready, 1)
            scan_input(Batch(0, 0))
            dve.wait_ge(plug_turned, 1)
            nc.vector.tensor_copy(patch_of[:, :, :],
                                  bank[6][:, 0:T * B].rearrange("p (t b) -> p b t", b=B)).then_inc(patches_ready, 1)
            step(nc.vector.tensor_scalar(far_f[:, 0, :], bank[5][0:1, 0:B], float(P), None, ALU.is_ge))
            step(nc.vector.tensor_tensor_scan(far_f[:, 1, :], ones_b[0:1, 0:B], far_f[:, 0, :], 0.0, ALU.mult, ALU.add))
            step(nc.vector.tensor_tensor(far_f[:, 2, :], far_f[:, 1, :], far_f[:, 0, :], ALU.subtract))
            nc.vector.tensor_copy(far_table[:, 0:B], far_f[:, 0, :]).then_inc(table_ready, 1)
            nc.vector.tensor_copy(far_table[:, B:2 * B], far_f[:, 2, :]).then_inc(table_ready, 1)
            dve.wait_ge(mus_loaded, 32)
            nc.vector.tensor_scalar(mus[:, 2:4, :], mus[:, 0:2, :], -1.0, 1.0, ALU.mult, ALU.add).then_inc(mus_ready, 1)
            for w in (WR, WK):
                weight_lo(w)
            dve.wait_ge(decay_hi_ready, 1)
            low(decay_lo[:, :, :], decay[:, :, :], f32(decay_hi[:, :, :])).then_inc(decay_lo_ready, 1)
            nc.vector.memset(turned[:, :, 0:1], 0.0).then_inc(zero_ready, 1)
            dve.wait_ge(mus_ready, 1)
            dve.wait_ge(zero_ready, 2)
            batches(dve, iteration, B)


_INS = ["x", "ctx_2048", "mask_BxS2_if0", "L0_xattn_W_in", "L0_xattn_b_in", "L0_xattn_g_res", "L0_xattn_g_init",
        "L0_ffn_W_r", "L0_ffn_W_k", "L0_ffn_W_v", "L0_ffn_mu_r", "L0_ffn_mu_k"]
_TURNED = {"L0_xattn_W_in", "L0_ffn_W_r", "L0_ffn_W_k", "L0_ffn_W_v"}


def layouts(inputs):
    arrays = {}
    for name in _INS:
        a = np.asarray(inputs[name])
        arrays[f"in_{name}"] = np.ascontiguousarray(a.T if name in _TURNED else a)
        if name == "x":
            arrays["in_x_turned"] = np.ascontiguousarray(a.transpose(0, 2, 1))
    return arrays


def kernel(**inputs):
    import concourse.bacc as bacc
    from concourse.bass_utils import run_bass_kernel_spmd

    nc = bacc.Bacc("TRN2", target_bir_lowering=False, num_devices=1)
    arrays = layouts(inputs)
    args = [nc.dram_tensor(name, a.shape, mybir.dt.from_np(a.dtype), kind="ExternalInput").ap()
            for name, a in arrays.items()]
    args.append(nc.dram_tensor("out_0", arrays["in_x"].shape, F32, kind="ExternalOutput").ap())
    build(nc, *args)
    r = run_bass_kernel_spmd(nc, [arrays], core_ids=[0])
    return r.results[0]["out_0"]
```

```python
import math
from contextlib import ExitStack

import numpy as np

import concourse.bass as bass
from concourse import mybir

F32 = mybir.dt.float32
F32R = mybir.dt.float32r
BF16 = mybir.dt.bfloat16
I32 = mybir.dt.int32
U32 = mybir.dt.uint32
ALU = mybir.AluOpType
ACT = mybir.ActivationFunctionType

P = 128
LN_EPS = 1e-5
RMS_EPS = 1e-5
EPSILON = 0.001
RING = 3


class Batch:

    def __init__(self, q, off):
        self.q, self.off = q + off // RING if isinstance(q, int) else q, off
        if isinstance(q, int):
            self.off = off % RING
        self.fixed = isinstance(q, int)
        self.slot = off % RING

    def number(self):
        return self.q * RING + self.off

    def plus(self, n):
        return Batch(self.q, self.off + n)

    def round(self):
        return self.q + self.off // RING

    def exists(self, count):
        return not self.fixed or 0 <= self.number() < count


def reached(eng, semaphore, batch, per_batch, done):
    value = batch.number() * per_batch + done
    if isinstance(value, int) and value <= 0:
        return
    eng.wait_ge(semaphore, value)


def hold(eng, passed):
    eng.sem_inc(passed, 1)


def batches(eng, iteration, count):
    rounds = (count - 4) // RING
    for n in range(-1, 1):
        iteration(Batch(0, n))
    with eng.Fori(0, rounds) as q:
        for off in range(1, RING + 1):
            iteration(Batch(q, off))
    for n in range(rounds * RING + 1, count):
        iteration(Batch(0, n))


def decay_powers():
    one = np.float32(1.0)
    dt = np.float32(-math.log(-math.expm1(float(np.float32(-EPSILON)))))
    a = np.float32(math.exp(-float(dt)))
    powers = [one]
    while powers[-1] * a > np.finfo(np.float32).tiny:
        powers.append(powers[-1] * a)
    return [float(p) for p in powers]


def build(nc, x, x_turned, ctx, patch_lens, w_in, b_in, g_res, g_init, w_r, w_k, w_v, mu_r, mu_k, out):
    B, S, D = x.shape
    DG = ctx.shape[2]
    C = D // P
    T = S // P
    H16, W32 = 16, 32
    LAST = B - 1
    SCAN = 3
    assert D == 512 and S == 512 and DG == 2 * D and B == 16 and H16 * W32 == S
    powers = decay_powers()
    input_gain = math.exp(-EPSILON)

    with ExitStack() as stack:
        def sb(name, shape, dt=F32):
            return stack.enter_context(nc.sbuf_tensor(name, shape, dt))

        def sem(name):
            return stack.enter_context(nc.semaphore(name))

        def sems(names):
            return [sem(name) for name in names.split()]

        bank = [stack.enter_context(nc.psum_tensor(f"bank{i}", [P, 512], F32)) for i in range(8)]

        mask_rows = nc.dram_tensor("mask_rows", [B, S], F32, kind="Internal").ap()
        s_rows = nc.dram_tensor("s_rows", [S, D], F32, kind="Internal").ap()

        wt_hi = [sb(f"w{n}_hi", [P, C, D], F32R) for n in "irkv"]
        wt_lo = [sb(f"w{n}_lo", [P, C, D], F32R) for n in "irkv"]
        WIN, WR, WK, WV = range(4)
        ring = [sb(f"ring{i}", [P, T, D]) for i in range(RING)]
        xt = sb("xt", [P, C, S])
        xt_hi, xt_lo = sb("xt_hi", [P, C, S], F32R), sb("xt_lo", [P, C, S], F32R)
        normed = sb("normed", [P, T, D])
        turned = sb("turned", [P, C, S + 1])
        xk_hi, xk_lo = sb("xk_hi", [P, C, S], F32R), sb("xk_lo", [P, C, S], F32R)
        xr_hi, xr_lo = sb("xr_hi", [P, C, S], F32R), sb("xr_lo", [P, C, S], F32R)
        gate = sb("gate", [P, T, D])
        scratch = sb("scratch", [P, 4, S])
        ctx_rows = sb("ctx_rows", [P, DG])
        u = sb("u", [P, D])
        u_hi, u_lo = sb("u_hi", [P, D], F32R), sb("u_lo", [P, D], F32R)
        scanned, far_scanned = sb("scanned", [P, D]), sb("far_scanned", [P, D])
        bias = sb("bias", [P, D])
        g_ctx = sb("g_ctx", [P, D])
        ident = sb("ident", [P, P])
        average = sb("average", [P, P])
        decay = sb("decay", [P, 2, P])
        decay_hi, decay_lo = sb("decay_hi", [P, 2, P], F32R), sb("decay_lo", [P, 2, P], F32R)
        mus = sb("mus", [P, 4, C])
        g_cols = sb("g_cols", [P, C])
        count_i = sb("count_i", [P, W32], I32)
        half = sb("half", [P, T])
        bn_a, mv_a, rs_a = (sb(f"{n}_a", [P, T, k]) for n, k in (("bn", 6), ("mv", 2), ("rs", 1)))
        v_a = sb("v_a", [P, RING, T])
        bn_b, mv_b, v_b, rs_b = (sb(f"{n}_b", [P, T, k]) for n, k in (("bn", 6), ("mv", 2), ("v", 1), ("rs", 1)))
        bn_c, mv_c, v_c, rs_c = (sb(f"{n}_c", [P, k]) for n, k in (("bn", 12), ("mv", 2), ("v", 2), ("rs", 1)))
        far_table = sb("far_table", [1, 2 * B], I32)
        far_f = sb("far_f", [1, 3, B])
        index_i = sb("index_i", [P, 3, T * B], I32)
        patch_of, patch_now = sb("patch_of", [P, B, T], U32), sb("patch_now", [P, T], U32)

        lens = [normed[0:B, 0:2, :].rearrange("p a b -> p (a b)").bitcast(I32),
                normed[0:B, 2:4, :].rearrange("p a b -> p (a b)").bitcast(I32)]
        index_f, index_s = u[0:B, :], far_scanned[0:B, :]
        mask = normed[0:H16, 0, :]
        mask_b, ones_b, sums_b, plug_b = (far_scanned[0:B, :], normed[0:B, 1, :], normed[0:B, 2, :], normed[0:B, 3, :])
        low_hot = scratch[:, 0:2, :].rearrange("p a b -> p (a b)").bitcast(BF16).rearrange("p (n w) -> p n w", w=W32)
        high_hot = scratch[:, 2, :].bitcast(BF16).rearrange("p (n h) -> p n h", h=H16)
        def f32(ap):
            return ap.bitcast(F32)

        staged = [gate, turned[:, :, 1:S + 1], ring[2], gate]

        lens_loaded, bias_loaded, g_ctx_loaded, mus_loaded, g_loaded = sems("lens_loaded bias_loaded g_ctx_loaded mus_loaded g_loaded")
        w_loaded = [sem(f"w_loaded{i}") for i in range(4)]
        x_loaded = [sem(f"x_loaded{i}") for i in range(RING)]
        xt_loaded, ctx_loaded = sems("xt_loaded ctx_loaded")
        half_ready, ident_ready, average_ready, counts_ready, decay_ready, decay_hi_ready, decay_lo_ready = sems(
            "half_ready ident_ready average_ready counts_ready decay_ready decay_hi_ready decay_lo_ready")
        zero_ready, ones_ready, zeros_ready, s_zeroed, g_ready, mus_ready = sems("zero_ready ones_ready zeros_ready s_zeroed g_ready mus_ready")
        pad_ready, plug_step, index_turned, hots_ready, mask_counted, mask_copied, mask_stored, mask_loaded = sems(
            "pad_ready plug_step index_turned hots_ready mask_counted mask_copied mask_stored mask_loaded")
        plug_turned, patches_ready, table_ready = sems("plug_turned patches_ready table_ready")
        g_applied, w_averaged, w_centred = sems("g_applied w_averaged w_centred")
        w_hi_ready, w_lo_ready = ([sem(f"w{n}_{part}_ready") for n in "irkv"] for part in ("hi", "lo"))
        bn_a_done, mv_a_done, v_a_done, rs_a_done, first_half_read = sems("bn_a_done mv_a_done v_a_done rs_a_done first_half_read")
        xt_hi_ready, xt_lo_ready, proj_done, x2_ready = sems("xt_hi_ready xt_lo_ready proj_done x2_ready")
        bn_c_done, mv_c_done, ms_c_done, v_c_done, rs_c_done = sems("bn_c_done mv_c_done ms_c_done v_c_done rs_c_done")
        u_ready, u_hi_ready, u_lo_ready, s_done, s_copied, s_stored, patch_picked, dep_added = sems(
            "u_ready u_hi_ready u_lo_ready s_done s_copied s_stored patch_picked dep_added")
        far_loaded, far_bn, far_mv, far_ms, far_v, far_rs, far_u, far_u_hi, far_u_lo = sems(
            "far_loaded far_bn far_mv far_ms far_v far_rs far_u far_u_hi far_u_lo")
        far_carried, far_s, far_copied, far_stored, far_over = sems("far_carried far_s far_copied far_stored far_over")
        bn_b_done, mv_b_done, v_b_done, rs_b_done, yn_ready, yn_turned, yt_ready = sems(
            "bn_b_done mv_b_done v_b_done rs_b_done yn_ready yn_turned yt_ready")
        carried, mixed, mix_hi_ready, mix_lo_ready = sems("carried mixed mix_hi_ready mix_lo_ready")
        r_done, gate_ready, k_done, relu_ready, square_ready, ka_hi_ready, ka_lo_ready = sems(
            "r_done gate_ready k_done relu_ready square_ready ka_hi_ready ka_lo_ready")
        v_done, gated, out_ready = sems("v_done gated out_ready")
        stored = [sem(f"stored{t}") for t in range(T)]
        dve_passed, pool_passed = sems("dve_passed pool_passed")

        def tile(t):
            return slice(t * P, (t + 1) * P)

        def is_first(b, n=0):
            return b.fixed and b.number() == n

        def is_last(b):
            return b.fixed and b.number() == LAST

        def ka(b):
            return (xt_hi, xt_lo) if is_last(b) else (xr_hi, xr_lo)

        def scan_bank(b):
            return bank[4 + SCAN if is_first(b, 1) else SCAN]

        def first_bank(b, t):
            return bank[4 + t if is_first(b) else t]

        def mix_row(b, i):
            return (1 - i // C if is_last(b) else i // C), i % C

        x_rows = x.rearrange("b (t p) d -> b p t d", p=P)
        xt_rows = x_turned.rearrange("b (c p) s -> b p c s", p=P)
        out_rows = out.rearrange("b (t p) d -> b p t d", p=P)

        def far_count(eng, b):
            n = b.number()
            return (eng.value_load(far_table[0:1, bass.ds(n, 1)], min_val=0, max_val=1),
                    eng.value_load(far_table[0:1, bass.ds(n + B, 1)], min_val=0, max_val=B - 1))

        SHIFTS = [1 << k for k in range(S.bit_length() - 1)]
        PAD = S // 2
        INDEX_STEP = len(SHIFTS) + 4
        PLUG_STEP = INDEX_STEP + 3 + 2

        block = stack.enter_context(nc.Block())

        @block.sync
        def _(sp):
            def load_w(w, rows):
                sp.dma_start(staged[w][:, :, :], rows.rearrange("(c p) d -> p c d", p=P)).then_inc(w_loaded[w], 16)

            def load_x(b):
                sp.dma_start(ring[b.slot][:, :, :], x_rows[b.number()]).then_inc(x_loaded[b.slot], 16)

            def load_xt(b):
                sp.dma_start(xt[:, :, :], xt_rows[b.number()]).then_inc(xt_loaded, 16)

            def load_ctx(b):
                sp.dma_start(ctx_rows[:, :], ctx[b.number(), 0:P, :]).then_inc(ctx_loaded, 16)

            sp.dma_start(lens[0][:, PAD:PAD + S], patch_lens).then_inc(lens_loaded, 16)
            load_w(WIN, w_in)
            load_xt(Batch(0, 0))
            load_ctx(Batch(0, 0))
            load_x(Batch(0, 0))
            load_w(WR, w_r)
            sp.wait_ge(mask_copied, 1)
            sp.dma_start(mask_rows.rearrange("b (h w) -> h b w", w=W32),
                         mask.rearrange("h (b w) -> h b w", w=W32)).then_inc(mask_stored, 16)
            sp.wait_ge(mask_stored, 16)
            sp.dma_start(mask_b, mask_rows).then_inc(mask_loaded, 16)
            reached(sp, xt_lo_ready, Batch(0, 0), 2, 2)
            load_xt(Batch(0, 1))
            reached(sp, s_stored, Batch(0, 0), 16, 16)
            load_x(Batch(0, 1))
            reached(sp, far_over, Batch(0, 0), 1, 1)
            load_ctx(Batch(0, 1))
            reached(sp, dep_added, Batch(0, 0), T * 16, T * 16)
            load_w(WK, w_k)
            sp.wait_ge(w_lo_ready[WIN], C)
            load_w(WV, w_v)

            def iteration(b):
                new = b.plus(2)
                if new.exists(B) and not is_first(new, 1):
                    reached(sp, xt_lo_ready, new.plus(-1), 2, 2)
                    load_xt(new)
                    reached(sp, out_ready, b.plus(-1), T, T)
                    if is_first(new, 2):
                        sp.wait_ge(w_lo_ready[WK], C)
                    load_x(new)
                    reached(sp, far_over, new.plus(-1), 1, 1)
                    load_ctx(new)
                if b.exists(B):
                    for t in range(T):
                        reached(sp, out_ready, b, T, t + 1)
                        sp.dma_start(out_rows[b.number(), :, t, :], gate[:, t, :]).then_inc(stored[t], 16)

            batches(sp, iteration, B)
            for t in range(T):
                sp.wait_ge(stored[t], 16 * B)

        @block.gpsimd
        def _(pool):
            nc.gpsimd.memset(scanned[:, :], 0.0).then_inc(zeros_ready, 1)
            for n in range(2):
                nc.gpsimd.memset(lens[n][:, 0:PAD], 0).then_inc(pad_ready, 1)
            nc.gpsimd.memset(half[:, :], -0.5).then_inc(half_ready, 1)
            nc.gpsimd.memset(average[:, :], 1.0 / D).then_inc(average_ready, 1)
            nc.gpsimd.memset(ident[:, :], 0.0).then_inc(ident_ready, 1)
            pool.wait_ge(ident_ready, 1)
            nc.gpsimd.affine_select(out=ident[:, :], in_=ident[:, :], compare_op=ALU.not_equal, fill=1.0, base=0,
                                    pattern=[[-1, P]], channel_multiplier=1).then_inc(ident_ready, 1)
            nc.gpsimd.iota(count_i[:, :], pattern=[[1, W32]], base=0, channel_multiplier=0).then_inc(counts_ready, 1)

            def make_decay():
                nc.gpsimd.memset(decay[:, :, :], 0.0).then_inc(decay_ready, 1)
                steps = 1
                for k, value in enumerate(powers):
                    for which, base in ((0, 0), (1, P)):
                        pool.wait_ge(decay_ready, max(steps - 1, 1))
                        nc.gpsimd.affine_select(out=decay[:, which, :], in_=decay[:, which, :],
                                                compare_op=ALU.not_equal, fill=value, base=base - k,
                                                pattern=[[1, P]], channel_multiplier=-1).then_inc(decay_ready, 1)
                        steps += 1

            def weight_lo(w, first=0, last=C):
                for c in range(first, last):
                    pool.wait_ge(w_hi_ready[w], c + 1)
                    nc.gpsimd.tensor_tensor(wt_lo[w][:, c, :], staged[w][:, c, :], f32(wt_hi[w][:, c, :]),
                                            ALU.subtract).then_inc(w_lo_ready[w], 1)

            def x_lo(b, n):
                reached(pool, xt_lo_ready, b, 2, n)
                reached(pool, xt_hi_ready, b, 2, n + 1)
                nc.gpsimd.tensor_tensor(xt_lo[:, 2 * n:2 * n + 2, :], xt[:, 2 * n:2 * n + 2, :],
                                        f32(xt_hi[:, 2 * n:2 * n + 2, :]), ALU.subtract).then_inc(xt_lo_ready, 1)

            def root_a(b):
                reached(pool, v_a_done, b, 1, 1)
                reached(pool, x2_ready, b.plus(-1), T, T)
                nc.gpsimd.tensor_tensor(rs_a[:, :, 0], v_a[:, b.slot, :], half[:, :], ALU.pow).then_inc(rs_a_done, 1)

            def root_b(b):
                reached(pool, v_b_done, b, 1, 1)
                reached(pool, yn_ready, b.plus(-1), T, T)
                nc.gpsimd.tensor_tensor(rs_b[:, :, 0], v_b[:, :, 0], half[:, :], ALU.pow).then_inc(rs_b_done, 1)

            def root_c(b):
                reached(pool, v_c_done, b, 1, 1)
                reached(pool, u_ready, b.plus(-1), 1, 1)
                nc.gpsimd.tensor_tensor(rs_c[:, :], v_c[:, 1:2], half[:, 0:1], ALU.pow).then_inc(rs_c_done, 1)

            def far(b):
                n = far_count(pool, b)
                with pool.If(n[0] > 0):
                    for c in range(1, T):
                        done = n[1] * (T - 1) + c
                        if c == 1:
                            reached(pool, u_ready, b, 1, 1)
                        else:
                            pool.wait_ge(far_u, done - 1)
                        hold(pool, pool_passed)
                        pool.dma_start(ctx_rows[:, :], ctx[b.number(), c * P:(c + 1) * P, :]).then_inc(far_loaded, 16)
                        pool.wait_ge(far_v, done)
                        nc.gpsimd.tensor_tensor(rs_c[:, :], v_c[:, 1:2], half[:, 0:1], ALU.pow).then_inc(far_rs, 1)
                        pool.wait_ge(far_copied, done)
                        hold(pool, pool_passed)
                        pool.dma_start(s_rows[c * P:(c + 1) * P, :],
                                       far_scanned[:, :]).then_inc(far_stored, 16)
                        pool.wait_ge(far_stored, done * 16)
                        hold(pool, pool_passed)

            def add_patches(b):
                if not is_first(b):
                    reached(pool, dep_added, b.plus(-1), T * 16, T * 16)
                nc.gpsimd.tensor_copy(patch_now[:, :], patch_of[:, bass.ds(b.number(), 1), :].rearrange("p a t -> p (a t)")
                                      ).then_inc(patch_picked, 1)
                reached(pool, bn_a_done, b, T, T)
                reached(pool, s_stored, b, 16, 16)
                reached(pool, patch_picked, b, 1, 1)
                hold(pool, pool_passed)
                for t in range(T):
                    pool.indirect_dma_start(ring[b.slot][:, t, :], None, s_rows[:, :],
                                            bass.IndirectOffsetOnAxis(ap=patch_now[:, t:t + 1], axis=0),
                                            compute_op=ALU.add).then_inc(dep_added, 16)

            def add_out(b, t):
                reached(pool, gated, b, T, t + 1)
                nc.gpsimd.tensor_tensor(gate[:, t, :], gate[:, t, :], ring[b.slot][:, t, :], ALU.add).then_inc(out_ready, 1)

            def iteration(b):
                nxt, new = b.plus(1), b.plus(2)
                if nxt.exists(B):
                    root_b(nxt)
                if is_first(b):
                    root_c(new)
                    root_a(new)
                elif new.exists(B) and not is_first(new, 1):
                    root_a(new)
                    root_c(new)
                if b.exists(B):
                    add_out(b, 0)
                    add_out(b, 1)
                if new.exists(B):
                    far(new)
                    add_patches(new)
                if is_first(nxt):
                    root_a(new)
                    weight_lo(WK)
                    weight_lo(WV)
                if b.exists(B):
                    add_out(b, 2)
                    add_out(b, 3)

            make_decay()
            pool.wait_ge(plug_step, INDEX_STEP)
            nc.gpsimd.memset(ones_b, 1.0).then_inc(ones_ready, 1)
            x_lo(Batch(0, 0), 0)
            pool.wait_ge(half_ready, 1)
            root_c(Batch(0, 0))
            x_lo(Batch(0, 0), 1)
            weight_lo(WIN)
            pool.wait_ge(table_ready, 2)
            pool.wait_ge(patches_ready, 1)
            pool.wait_ge(s_zeroed, 16 * (T - 1))
            far(Batch(0, 0))
            add_patches(Batch(0, 0))
            root_a(Batch(0, 0))
            weight_lo(WR, 0, C // 2)
            root_c(Batch(0, 1))
            x_lo(Batch(0, 1), 1)
            weight_lo(WR, C // 2, C)
            batches(pool, iteration, B)

        @block.tensor
        def _(pe):
            def product(where, lhs_hi, lhs_lo, rhs_hi, rhs_lo, start, stop):
                nc.tensor.matmul(where, lhs_hi, rhs_hi, start=start, stop=False)
                nc.tensor.matmul(where, lhs_hi, rhs_lo, start=False, stop=False)
                return nc.tensor.matmul(where, lhs_lo, rhs_hi, start=False, stop=stop)

            def project_tile(b, t, c):
                last = product(first_bank(b, t)[:, :], xt_hi[:, c, tile(t)], xt_lo[:, c, tile(t)],
                               wt_hi[WIN][:, c, :], wt_lo[WIN][:, c, :], c == 0, c == C - 1)
                if c == C - 1:
                    last.then_inc(proj_done, 1)
                elif is_first(b) and c == C // 2 - 1 and t == T - 1:
                    last.then_inc(first_half_read, 1)

            def project(b):
                for t in range(T):
                    reached(pe, yt_ready, b.plus(-1), T, t + 1)
                    if t == 0:
                        reached(pe, xt_lo_ready, b, 2, 2)
                    for c in range(C):
                        project_tile(b, t, c)

            def scan(b):
                reached(pe, u_lo_ready, b, 1, 1)
                product(scan_bank(b)[:, :], decay_hi[:, 0, :], decay_lo[:, 0, :], u_hi[:, :], u_lo[:, :],
                        True, True).then_inc(s_done, 1)

            def far(b):
                n = far_count(pe, b)
                with pe.If(n[0] > 0):
                    for c in range(1, T):
                        done = n[1] * (T - 1) + c
                        if c > 1:
                            pe.wait_ge(far_copied, done - 1)
                        else:
                            reached(pe, s_copied, b, 1, 1)
                        product(scan_bank(b)[:, :], decay_hi[:, 1, :], decay_lo[:, 1, :], u_hi[:, :], u_lo[:, :],
                                True, False).then_inc(far_carried, 1)
                        pe.wait_ge(far_u_lo, done)
                        product(scan_bank(b)[:, :], decay_hi[:, 0, :], decay_lo[:, 0, :], u_hi[:, :], u_lo[:, :],
                                False, True).then_inc(far_s, 1)

            def gate_product(b):
                order = [(t, c) for t in range(T) for c in range(C)]
                if is_first(b):
                    order = [(t, c) for c in range(C) for t in range(T)]
                for t, c in order:
                    if c == 0:
                        reached(pe, gated, b.plus(-1), T, t + 1)
                    if t == 0:
                        reached(pe, mix_lo_ready, b, 2 * C, c + 1 + (C if is_last(b) else 0))
                        if is_first(b):
                            pe.wait_ge(w_lo_ready[WR], C)
                    last = product(bank[4 + t][:, :], xr_hi[:, c, tile(t)], xr_lo[:, c, tile(t)],
                                   wt_hi[WR][:, c, :], wt_lo[WR][:, c, :], c == 0, c == C - 1)
                    if c == C - 1:
                        last.then_inc(r_done, 1)

            def key_product(b):
                for m in range(C):
                    if is_first(b):
                        pe.wait_ge(w_lo_ready[WK], C)
                    if is_last(b):
                        reached(pe, yt_ready, b, T, T)
                    else:
                        reached(pe, x2_ready, b.plus(1), T, m + 1)
                    for c in range(C):
                        if m == 0:
                            reached(pe, mix_lo_ready, b, 2 * C, c + 1 + (0 if is_last(b) else C))
                        last = product(bank[m][:, :], wt_hi[WK][:, c, tile(m)], wt_lo[WK][:, c, tile(m)],
                                       xk_hi[:, c, :], xk_lo[:, c, :], c == 0, c == C - 1)
                    last.then_inc(k_done, 1)

            def value_product(b, t, first, last):
                ka_hi, ka_lo = ka(b)
                if first == 0:
                    reached(pe, gate_ready, b, T, t + 1)
                    if is_first(b) and t == 0:
                        pe.wait_ge(w_lo_ready[WV], C)
                for m in range(first, last):
                    if t == 0:
                        reached(pe, ka_lo_ready, b, C, m + 1)
                    done = product(bank[4 + t][:, :], ka_hi[:, m, tile(t)], ka_lo[:, m, tile(t)],
                                   wt_hi[WV][:, m, :], wt_lo[WV][:, m, :], m == 0, m == C - 1)
                if last == C:
                    done.then_inc(v_done, 1)

            def turn(b):
                for t in range(T):
                    reached(pe, yn_ready, b, T, t + 1)
                    if b.plus(-1).exists(B):
                        reached(pe, relu_ready, b.plus(-1), C, t + 1)
                    if t == SCAN and b.plus(1).exists(B):
                        reached(pe, s_copied, b.plus(1), 1, 1)
                        reached(pe, far_over, b.plus(1), 1, 1)
                    for c in range(C):
                        last = nc.tensor.transpose(first_bank(b, t)[:, tile(c)], normed[:, t, c * P:(c + 1) * P],
                                                   ident[:, :])
                    last.then_inc(yn_turned, 1)

            def iteration(b):
                nxt, new = b.plus(1), b.plus(2)
                if is_first(nxt):
                    first_steps(new)
                    return
                if nxt.exists(B) and not is_first(nxt, 1):
                    project(nxt)
                if b.exists(B) and not is_last(b):
                    gate_product(b)
                    key_product(b)
                    if is_last(nxt):
                        turn(nxt)
                    value_product(b, 0, 0, C - 1)
                    value_product(b, 1, 0, C - 1)
                    value_product(b, 0, C - 1, C)
                    value_product(b, 1, C - 1, C)
                if is_last(b):
                    key_product(b)
                    gate_product(b)
                    for t in range(T):
                        value_product(b, t, 0, C)
                if new.exists(B):
                    scan(new)
                    far(new)
                if b.exists(B) and not is_last(b):
                    for t in range(2, T):
                        value_product(b, t, 0, C)
                if nxt.exists(B) and not is_last(nxt):
                    turn(nxt)

            def first_steps(b):
                reached(pe, far_over, b.plus(-1), 1, 1)
                for c in range(C):
                    reached(pe, xt_lo_ready, b, 2, c // 2 + 1)
                    for t in range(T - 1):
                        project_tile(b, t, c)
                reached(pe, x2_ready, b.plus(-1), T, T)
                scan(b)
                far(b)
                turn(b.plus(-1))
                for c in range(C):
                    project_tile(b, T - 1, c)

            def average_chunk(c):
                pe.wait_ge(g_applied, c + 1)
                return nc.tensor.matmul(bank[2][:, :], average[:, :], staged[WIN][:, c, :], start=c == 0, stop=c == C - 1)

            pe.wait_ge(average_ready, 1)
            for c in range(C // 2):
                average_chunk(c)
            pe.wait_ge(ident_ready, 2)
            pe.wait_ge(plug_step, INDEX_STEP)
            for j in range(T):
                last = nc.tensor.transpose(bank[1][:, j * B:(j + 1) * B], index_f[:, tile(j)], ident[0:B, 0:B])
            last.then_inc(index_turned, 1)
            for c in range(C // 2, C):
                last = average_chunk(c)
            last.then_inc(w_averaged, 1)
            pe.wait_ge(hots_ready, 2)
            for n in range(B):
                for j in range(T):
                    last = nc.tensor.matmul(bank[0][0:H16, n * W32:(n + 1) * W32], high_hot[:, j * B + n, :],
                                            low_hot[:, j * B + n, :], start=j == 0, stop=j == T - 1)
            last.then_inc(mask_counted, 1)
            pe.wait_ge(decay_lo_ready, 1)
            scan(Batch(0, 0))
            for c in range(C):
                reached(pe, xt_lo_ready, Batch(0, 0), 2, c // 2 + 1)
                pe.wait_ge(w_lo_ready[WIN], c + 1)
                for t in range(T):
                    project_tile(Batch(0, 0), t, c)
                    if c == 0 and t == 1:
                        pe.wait_ge(plug_step, PLUG_STEP)
                        for j in range(T):
                            nc.tensor.transpose(bank[0][:, j * B:(j + 1) * B], plug_b[:, tile(j)], ident[0:B, 0:B])
                        nc.tensor.matmul(bank[1][0:1, 0:B], plug_b[:, S - 1:S], ident[0:B, 0:B], start=True,
                                         stop=True).then_inc(plug_turned, 1)
                if c == 2:
                    pe.wait_ge(table_ready, 2)
                    far(Batch(0, 0))

            batches(pe, iteration, B)

        @block.scalar
        def _(act):
            def copy(to, of):
                return nc.scalar.activation(to, of, ACT.Copy)

            def weight_hi(w):
                for c in range(C):
                    if w == WIN:
                        act.wait_ge(w_centred, c + 1)
                    else:
                        act.wait_ge(w_loaded[w], 16)
                    copy(wt_hi[w][:, c, :], staged[w][:, c, :]).then_inc(w_hi_ready[w], 1)

            def x_hi(b, n):
                reached(act, xt_loaded, b, 16, 16)
                if is_first(b, 1) and n == 0:
                    act.wait_ge(first_half_read, 1)
                else:
                    reached(act, proj_done, b.plus(-1), T, T)
                copy(xt_hi[:, 2 * n:2 * n + 2, :], xt[:, 2 * n:2 * n + 2, :]).then_inc(xt_hi_ready, 1)

            def u_high(b):
                reached(act, u_ready, b, 1, 1)
                reached(act, far_over, b.plus(-1), 1, 1)
                reached(act, s_done, b.plus(-1), 1, 1)
                copy(u_hi[:, :], u[:, :]).then_inc(u_hi_ready, 1)

            def store_scan(b):
                reached(act, s_copied, b, 1, 1)
                reached(act, dep_added, b.plus(-1), T * 16, T * 16)
                act.dma_start(s_rows[0:P, :], scanned[:, :]).then_inc(s_stored, 16)

            def mix_hi(b, first, last):
                for i in range(first, last):
                    which, c = mix_row(b, i)
                    reached(act, mixed, b, 2 * C, i + 1)
                    if i == 0:
                        reached(act, k_done, b.plus(-1), C, C)
                    if which == 0 and c == 0:
                        reached(act, v_done, b.plus(-1), T, T)
                    copy((xr_hi, xk_hi)[which][:, c, :], scratch[:, 2 + i % 2, :]).then_inc(mix_hi_ready, 1)

            def gates(b):
                for t in range(T):
                    reached(act, r_done, b, T, t + 1)
                    reached(act, stored[t], b, 16, 0)
                    if is_first(b):
                        act.wait_ge(w_lo_ready[WV], C)
                    nc.scalar.activation(gate[:, t, :], bank[4 + t][:, :], ACT.Sigmoid).then_inc(gate_ready, 1)

            def squares(b):
                for m in range(C):
                    reached(act, k_done, b, C, m + 1)
                    if m == 0:
                        reached(act, mix_lo_ready, b, 2 * C, 2 * C)
                    if m >= 2:
                        reached(act, ka_lo_ready, b, C, m - 1)
                    nc.scalar.activation(scratch[:, m % 2, :], bank[m][:, :], ACT.Relu).then_inc(relu_ready, 1)
                    reached(act, relu_ready, b, C, m + 1)
                    nc.scalar.activation(scratch[:, 2 + m % 2, :], scratch[:, m % 2, :], ACT.Square).then_inc(square_ready, 1)
                    reached(act, square_ready, b, C, m + 1)
                    copy(ka(b)[0][:, m, :], scratch[:, 2 + m % 2, :]).then_inc(ka_hi_ready, 1)

            def turned_out(b):
                for t in range(T):
                    reached(act, yn_turned, b, T, t + 1)
                    if t == 0:
                        reached(act, mix_lo_ready, b.plus(-1), 2 * C, 2 * C)
                        if is_first(b):
                            act.wait_ge(w_lo_ready[WR], C)
                    copy(turned[:, :, 1 + t * P:1 + (t + 1) * P],
                         first_bank(b, t)[:, :].rearrange("p (c n) -> p c n", c=C)).then_inc(yt_ready, 1)

            def iteration(b):
                nxt, new = b.plus(1), b.plus(2)
                if b.exists(B):
                    if is_last(b):
                        mix_hi(b, C, 2 * C)
                        squares(b)
                        gates(b)
                    else:
                        mix_hi(b, 0, 2 * C)
                        gates(b)
                if is_first(b):
                    squares(b)
                    u_high(new)
                if new.exists(B) and not is_first(new, 1):
                    x_hi(new, 0)
                    x_hi(new, 1)
                if b.exists(B) and not is_last(b) and not is_first(b):
                    squares(b)
                if is_last(nxt):
                    turned_out(nxt)
                    mix_hi(nxt, 0, C)
                if is_first(nxt):
                    x_hi(new, 1)
                    u_high(new)
                    weight_hi(WK)
                    store_scan(new)
                    weight_hi(WV)
                    turned_out(nxt)
                elif new.exists(B):
                    if not is_first(b):
                        u_high(new)
                    store_scan(new)
                if nxt.exists(B) and not is_last(nxt) and not is_first(nxt):
                    turned_out(nxt)

            act.dma_start(g_cols[:, :], g_res.rearrange("(c p) -> p c", p=P),
                          allow_slow_non_contiguous=True).then_inc(g_loaded, 16)
            act.dma_start(bias[:, :], b_in.partition_broadcast(P)).then_inc(bias_loaded, 16)
            act.dma_start(g_ctx[:, :], g_init[0:D].partition_broadcast(P)).then_inc(g_ctx_loaded, 16)
            for n, mu in enumerate((mu_r, mu_k)):
                act.dma_start(mus[:, n, :], mu.rearrange("(c p) -> p c", p=P),
                              allow_slow_non_contiguous=True).then_inc(mus_loaded, 16)
            act.wait_ge(zeros_ready, 1)
            copy(turned[:, :, 0:1], scanned[:, 0:C].unsqueeze(2)).then_inc(zero_ready, 1)
            for n in range(1, T):
                act.dma_start(s_rows[tile(n), :], scanned[:, :]).then_inc(s_zeroed, 16)
            act.wait_ge(g_loaded, 16)
            act.wait_ge(w_loaded[WIN], 16)
            for c in range(C):
                nc.scalar.activation(staged[WIN][:, c, :], staged[WIN][:, c, :], ACT.Copy,
                                     scale=g_cols[:, c:c + 1]).then_inc(g_applied, 1)
            x_hi(Batch(0, 0), 0)
            x_hi(Batch(0, 0), 1)
            act.wait_ge(g_ctx_loaded, 16)
            nc.scalar.activation(g_ctx[:, :], g_ctx[:, :], ACT.Copy, scale=input_gain).then_inc(g_ready, 1)
            act.wait_ge(decay_ready, 2 * len(powers) + 1)
            copy(decay_hi[:, :, :], decay[:, :, :]).then_inc(decay_hi_ready, 1)
            u_high(Batch(0, 0))
            weight_hi(WIN)
            store_scan(Batch(0, 0))
            weight_hi(WR)
            x_hi(Batch(0, 1), 0)
            batches(act, iteration, B)

        @block.vector
        def _(dve):
            steps = [0]

            def step(instruction):
                instruction.then_inc(plug_step, 1)
                steps[0] += 1
                dve.wait_ge(plug_step, steps[0])

            def low(to, whole, high):
                return nc.vector.tensor_tensor(to, whole, high, ALU.subtract)

            def u_low(b):
                reached(dve, u_hi_ready, b, 1, 1)
                low(u_lo[:, :], u[:, :], f32(u_hi[:, :])).then_inc(u_lo_ready, 1)

            def scan_out(b):
                reached(dve, s_done, b, 1, 1)
                reached(dve, s_stored, b, 16, 0)
                nc.vector.tensor_tensor(scanned[:, :], scan_bank(b)[:, :], bias[:, :], ALU.add).then_inc(s_copied, 1)

            def x_lo(b, n):
                reached(dve, xt_hi_ready, b, 2, n + 1)
                low(xt_lo[:, 2 * n:2 * n + 2, :], xt[:, 2 * n:2 * n + 2, :],
                    f32(xt_hi[:, 2 * n:2 * n + 2, :])).then_inc(xt_lo_ready, 1)

            def statistics_a(b, t):
                dve.wait_ge(x_loaded[b.slot], (b.round() + 1) * 16)
                nc.vector.bn_stats(bn_a[:, t, :], ring[b.slot][:, t, :]).then_inc(bn_a_done, 1)

            def stats_a(b, first=0):
                for t in range(first, T):
                    statistics_a(b, t)
                reached(dve, bn_a_done, b, T, T)
                hold(dve, dve_passed)
                for t in range(T):
                    nc.vector.bn_aggr(mv_a[:, t, :], bn_a[:, t, :]).then_inc(mv_a_done, 1)
                reached(dve, mv_a_done, b, T, T)
                nc.vector.tensor_scalar(v_a[:, b.slot, :], mv_a[:, :, 1], 1.0 + RMS_EPS, RMS_EPS * LN_EPS,
                                        ALU.mult, ALU.add).then_inc(v_a_done, 1)

            def stats_c(b):
                reached(dve, ctx_loaded, b, 16, 16)
                for h in range(2):
                    nc.vector.bn_stats(bn_c[:, 6 * h:6 * h + 6], ctx_rows[:, h * D:(h + 1) * D]).then_inc(bn_c_done, 1)
                reached(dve, bn_c_done, b, 2, 2)
                hold(dve, dve_passed)
                nc.vector.bn_aggr(mv_c[:, :], bn_c[:, :]).then_inc(mv_c_done, 1)
                reached(dve, mv_c_done, b, 1, 1)
                nc.vector.scalar_tensor_tensor(v_c[:, 0:1], mv_c[:, 0:1], mv_c[:, 0:1], mv_c[:, 1:2],
                                               ALU.mult, ALU.add).then_inc(ms_c_done, 1)
                reached(dve, ms_c_done, b, 1, 1)
                nc.vector.tensor_scalar(v_c[:, 1:2], v_c[:, 0:1], RMS_EPS, None, ALU.add).then_inc(v_c_done, 1)

            def scan_input(b):
                reached(dve, rs_c_done, b, 1, 1)
                reached(dve, u_lo_ready, b.plus(-1), 1, 1)
                nc.vector.scalar_tensor_tensor(u[:, :], ctx_rows[:, 0:D], rs_c[:, :], g_ctx[:, :],
                                               ALU.mult, ALU.mult).then_inc(u_ready, 1)

            def far(b):
                n = far_count(dve, b)
                with dve.If(n[0] > 0):
                    for c in range(1, T):
                        done = n[1] * (T - 1) + c
                        dve.wait_ge(far_loaded, done * 16)
                        for h in range(2):
                            nc.vector.bn_stats(bn_c[:, 6 * h:6 * h + 6], ctx_rows[:, h * D:(h + 1) * D]).then_inc(far_bn, 1)
                        dve.wait_ge(far_bn, done * 2)
                        hold(dve, dve_passed)
                        nc.vector.bn_aggr(mv_c[:, :], bn_c[:, :]).then_inc(far_mv, 1)
                        dve.wait_ge(far_mv, done)
                        nc.vector.scalar_tensor_tensor(v_c[:, 0:1], mv_c[:, 0:1], mv_c[:, 0:1], mv_c[:, 1:2],
                                                       ALU.mult, ALU.add).then_inc(far_ms, 1)
                        dve.wait_ge(far_ms, done)
                        nc.vector.tensor_scalar(v_c[:, 1:2], v_c[:, 0:1], RMS_EPS, None, ALU.add).then_inc(far_v, 1)
                        dve.wait_ge(far_rs, done)
                        nc.vector.scalar_tensor_tensor(u[:, :], ctx_rows[:, 0:D], rs_c[:, :], g_ctx[:, :],
                                                       ALU.mult, ALU.mult).then_inc(far_u, 1)
                        dve.wait_ge(far_u, done)
                        dve.wait_ge(far_carried, done)
                        nc.vector.tensor_copy(u_hi[:, :], u[:, :]).then_inc(far_u_hi, 1)
                        dve.wait_ge(far_u_hi, done)
                        low(u_lo[:, :], u[:, :], f32(u_hi[:, :])).then_inc(far_u_lo, 1)
                        dve.wait_ge(far_s, done)
                        if c > 1:
                            dve.wait_ge(far_stored, (done - 1) * 16)
                        nc.vector.tensor_tensor(far_scanned[:, :], scan_bank(b)[:, :], bias[:, :],
                                                ALU.add).then_inc(far_copied, 1)
                    dve.wait_ge(far_copied, n[1] * (T - 1) + T - 1)
                    hold(dve, dve_passed)

            def carry(b, i):
                which, c = mix_row(b, i)
                nc.vector.tensor_scalar(scratch[:, i % 2, :], turned[:, c, 0:S], mus[:, 2 + which, c:c + 1], None,
                                        ALU.mult).then_inc(carried, 1)

            def mix(b, i):
                which, c = mix_row(b, i)
                reached(dve, carried, b, 2 * C, i + 1)
                nc.vector.scalar_tensor_tensor(scratch[:, 2 + i % 2, :], turned[:, c, 1:S + 1],
                                               mus[:, which, c:c + 1], scratch[:, i % 2, :],
                                               ALU.mult, ALU.add).then_inc(mixed, 1)

            def mix_low(b, i):
                which, c = mix_row(b, i)
                reached(dve, mix_hi_ready, b, 2 * C, i + 1)
                hi, lo = ((xr_hi, xr_lo), (xk_hi, xk_lo))[which]
                low(lo[:, c, :], scratch[:, 2 + i % 2, :], f32(hi[:, c, :])).then_inc(mix_lo_ready, 1)

            def mixing(b, first, last):
                for i in range(first, last):
                    if i == 0:
                        reached(dve, yt_ready, b, T, T)
                        carry(b, 0)
                    else:
                        reached(dve, mixed, b, 2 * C, i)
                    if i + 1 < 2 * C and not (is_first(b) and i == 0):
                        carry(b, i + 1)
                    if i >= 2:
                        reached(dve, mix_lo_ready, b, 2 * C, i - 1)
                    mix(b, i)
                    if is_first(b) and i == 0:
                        carry(b, i + 1)
                        mix_low(b, i)
                        continue
                    if i >= (2 if is_first(b) else 1):
                        mix_low(b, i - 1)
                if last == 2 * C:
                    mix_low(b, last - 1)

            def add_x(b, t):
                reached(dve, proj_done, b, T, t + 1)
                if t == 0:
                    reached(dve, dep_added, b, T * 16, T * 16)
                    reached(dve, rs_a_done, b, 1, 1)
                nc.vector.scalar_tensor_tensor(ring[b.slot][:, t, :], first_bank(b, t)[:, :], rs_a[:, t, :],
                                               ring[b.slot][:, t, :], ALU.mult, ALU.add).then_inc(x2_ready, 1)

            def stats_b(b):
                for t in range(T):
                    reached(dve, x2_ready, b, T, t + 1)
                    nc.vector.bn_stats(bn_b[:, t, :], ring[b.slot][:, t, :]).then_inc(bn_b_done, 1)
                reached(dve, bn_b_done, b, T, T)
                hold(dve, dve_passed)
                for t in range(T):
                    nc.vector.bn_aggr(mv_b[:, t, :], bn_b[:, t, :]).then_inc(mv_b_done, 1)
                reached(dve, mv_b_done, b, T, T)
                nc.vector.tensor_scalar(v_b[:, :, 0], mv_b[:, :, 1], LN_EPS, None, ALU.add).then_inc(v_b_done, 1)

            def norm_b(b):
                reached(dve, rs_b_done, b, 1, 1)
                reached(dve, yn_turned, b.plus(-1), T, T)
                for t in range(T):
                    nc.vector.tensor_scalar(normed[:, t, :], ring[b.slot][:, t, :], mv_b[:, t, 0:1], rs_b[:, t, :],
                                            ALU.subtract, ALU.mult).then_inc(yn_ready, 1)

            def gating(b, t):
                reached(dve, v_done, b, T, t + 1)
                reached(dve, gate_ready, b, T, t + 1)
                nc.vector.tensor_tensor(gate[:, t, :], bank[4 + t][:, :], gate[:, t, :], ALU.mult).then_inc(gated, 1)

            def ka_low(b, m):
                ka_hi, ka_lo = ka(b)
                reached(dve, ka_hi_ready, b, C, m + 1)
                low(ka_lo[:, m, :], scratch[:, 2 + m % 2, :], f32(ka_hi[:, m, :])).then_inc(ka_lo_ready, 1)

            def iteration(b):
                nxt, new = b.plus(1), b.plus(2)
                if is_first(nxt):
                    for t in range(T):
                        add_x(nxt, t)
                        if t == 0:
                            scan_input(new)
                        if t == 2:
                            u_low(new)
                    stats_b(nxt)
                    scan_out(new)
                    far(new)
                    dve.sem_inc(far_over, 1)
                    norm_b(nxt)
                    stats_a(new, 2)
                    return
                if b.exists(B):
                    mixing(b, C if is_last(b) else 0, 2 * C if is_last(b) else C + 1)
                if nxt.exists(B):
                    add_x(nxt, 0)
                    add_x(nxt, 1)
                if b.exists(B) and not is_last(b):
                    mixing(b, C + 1, 2 * C - 1)
                if nxt.exists(B):
                    add_x(nxt, 2)
                if b.exists(B) and not is_last(b):
                    mixing(b, 2 * C - 1, 2 * C)
                if nxt.exists(B):
                    add_x(nxt, 3)
                    stats_b(nxt)
                if is_first(b):
                    ka_low(b, 0)
                    stats_c(new)
                    ka_low(b, 1)
                    scan_input(new)
                    ka_low(b, 2)
                    stats_a(new)
                    ka_low(b, 3)
                    u_low(new)
                    norm_b(nxt)
                    gating(b, 0)
                    gating(b, 1)
                    x_lo(new, 0)
                    x_lo(new, 1)
                    scan_out(new)
                    far(new)
                    dve.sem_inc(far_over, 1)
                    gating(b, 2)
                    gating(b, 3)
                    return
                if new.exists(B):
                    stats_a(new)
                    stats_c(new)
                if nxt.exists(B):
                    norm_b(nxt)
                for m in range(C):
                    if b.exists(B):
                        ka_low(b, m)
                    if new.exists(B):
                        if m in (1, 2):
                            x_lo(new, m - 1)
                        if m == 2:
                            scan_input(new)
                if is_last(nxt):
                    mixing(nxt, 0, C)
                if new.exists(B):
                    u_low(new)
                if b.exists(B):
                    gating(b, 0)
                    gating(b, 1)
                if new.exists(B):
                    scan_out(new)
                    far(new)
                    dve.sem_inc(far_over, 1)
                if b.exists(B):
                    gating(b, 2)
                    gating(b, 3)

            dve.wait_ge(lens_loaded, 16)
            dve.wait_ge(pad_ready, 2)
            here, there = lens
            for shift in SHIFTS:
                step(nc.vector.tensor_tensor(there[:, PAD:PAD + S], here[:, PAD:PAD + S],
                                             here[:, PAD - shift:PAD + S - shift], ALU.add))
                here, there = there, here
            step(nc.vector.tensor_scalar(index_f, here[:, PAD:PAD + S], -1.0, None, ALU.add))
            step(nc.vector.tensor_scalar(index_s, index_f, 0.0, float(S), ALU.is_lt, ALU.mult))
            step(nc.vector.tensor_tensor(index_s, index_f, index_s, ALU.add))
            step(nc.vector.tensor_scalar(index_f, index_s, -1.0, float(2 * S - 1), ALU.max, ALU.min))
            assert steps[0] == INDEX_STEP

            dve.wait_ge(counts_ready, 1)
            dve.wait_ge(index_turned, 1)
            step(nc.vector.tensor_copy(index_i[:, 0, :], bank[1][:, 0:T * B]))
            step(nc.vector.tensor_scalar(index_i[:, 1, :], index_i[:, 0, :], 5, None, ALU.arith_shift_right))
            step(nc.vector.tensor_scalar(index_i[:, 2, :], index_i[:, 0, :], W32 - 1, None, ALU.bitwise_and))
            nc.vector.tensor_tensor(high_hot, index_i[:, 1, :].unsqueeze(2).to_broadcast([P, T * B, H16]),
                                    count_i[:, 0:H16].unsqueeze(1).to_broadcast([P, T * B, H16]),
                                    ALU.is_equal).then_inc(hots_ready, 1)
            nc.vector.tensor_tensor(low_hot, index_i[:, 2, :].unsqueeze(2).to_broadcast([P, T * B, W32]),
                                    count_i[:, :].unsqueeze(1).to_broadcast([P, T * B, W32]),
                                    ALU.is_equal).then_inc(hots_ready, 1)

            stats_c(Batch(0, 0))
            dve.wait_ge(mask_counted, 1)
            nc.vector.tensor_scalar(mask, bank[0][0:H16, :], 1.0, None, ALU.min).then_inc(mask_copied, 1)
            dve.wait_ge(g_ready, 1)
            scan_input(Batch(0, 0))
            dve.wait_ge(decay_hi_ready, 1)
            low(decay_lo[:, :, :], decay[:, :, :], f32(decay_hi[:, :, :])).then_inc(decay_lo_ready, 1)
            dve.wait_ge(w_averaged, 1)
            for c in range(C):
                nc.vector.tensor_tensor(staged[WIN][:, c, :], staged[WIN][:, c, :], bank[2][:, :],
                                        ALU.subtract).then_inc(w_centred, 1)
                if c == 0:
                    u_low(Batch(0, 0))
                if c == 2:
                    dve.wait_ge(bias_loaded, 16)
                    dve.wait_ge(s_zeroed, 16 * (T - 1))
                    scan_out(Batch(0, 0))
            dve.wait_ge(mask_loaded, 16)
            dve.wait_ge(ones_ready, 1)
            step(nc.vector.tensor_tensor_scan(sums_b, ones_b, mask_b, 0.0, ALU.mult, ALU.add))
            step(nc.vector.tensor_scalar(plug_b, sums_b, -1.0, 0.0, ALU.add, ALU.max))
            assert steps[0] == PLUG_STEP
            statistics_a(Batch(0, 0), 0)
            dve.wait_ge(plug_turned, 1)
            nc.vector.tensor_copy(patch_of[:, :, :],
                                  bank[0][:, 0:T * B].rearrange("p (t b) -> p b t", b=B)).then_inc(patches_ready, 1)
            step(nc.vector.tensor_scalar(far_f[:, 0, :], bank[1][0:1, 0:B], float(P), None, ALU.is_ge))
            step(nc.vector.tensor_tensor_scan(far_f[:, 1, :], ones_b[0:1, 0:B], far_f[:, 0, :], 0.0, ALU.mult, ALU.add))
            step(nc.vector.tensor_tensor(far_f[:, 2, :], far_f[:, 1, :], far_f[:, 0, :], ALU.subtract))
            nc.vector.tensor_copy(far_table[:, 0:B], far_f[:, 0, :]).then_inc(table_ready, 1)
            nc.vector.tensor_copy(far_table[:, B:2 * B], far_f[:, 2, :]).then_inc(table_ready, 1)
            stats_a(Batch(0, 0), 1)
            dve.wait_ge(table_ready, 2)
            far(Batch(0, 0))
            dve.sem_inc(far_over, 1)
            dve.wait_ge(mus_loaded, 32)
            nc.vector.tensor_scalar(mus[:, 2:4, :], mus[:, 0:2, :], -1.0, 1.0, ALU.mult, ALU.add).then_inc(mus_ready, 1)
            dve.wait_ge(mus_ready, 1)
            dve.wait_ge(zero_ready, 1)
            x_lo(Batch(0, 1), 0)
            statistics_a(Batch(0, 1), 0)
            statistics_a(Batch(0, 1), 1)
            stats_c(Batch(0, 1))
            batches(dve, iteration, B)


_INS = ["x", "ctx_2048", "mask_BxS2_if0", "L0_xattn_W_in", "L0_xattn_b_in", "L0_xattn_g_res", "L0_xattn_g_init",
        "L0_ffn_W_r", "L0_ffn_W_k", "L0_ffn_W_v", "L0_ffn_mu_r", "L0_ffn_mu_k"]
_TURNED = {"L0_xattn_W_in", "L0_ffn_W_r", "L0_ffn_W_k", "L0_ffn_W_v"}


def layouts(inputs):
    arrays = {}
    for name in _INS:
        a = np.asarray(inputs[name])
        arrays[f"in_{name}"] = np.ascontiguousarray(a.T if name in _TURNED else a)
        if name == "x":
            arrays["in_x_turned"] = np.ascontiguousarray(a.transpose(0, 2, 1))
    return arrays


def kernel(**inputs):
    import concourse.bacc as bacc
    from concourse.bass_utils import run_bass_kernel_spmd

    nc = bacc.Bacc("TRN2", target_bir_lowering=False, num_devices=1)
    arrays = layouts(inputs)
    args = [nc.dram_tensor(name, a.shape, mybir.dt.from_np(a.dtype), kind="ExternalInput").ap()
            for name, a in arrays.items()]
    args.append(nc.dram_tensor("out_0", arrays["in_x"].shape, F32, kind="ExternalOutput").ap())
    build(nc, *args)
    r = run_bass_kernel_spmd(nc, [arrays], core_ids=[0])
    return r.results[0]["out_0"]
```
